# Optimizing a Trainium2 kernel written in Bass

```python
import numpy as np
import jax
import jax.numpy as jnp

def _softmax(x, axis=-1):
    return jax.nn.softmax(x, axis=axis)
def _gelu(x):
    return jax.nn.gelu(x, approximate=True)
def _silu(x):
    return jax.nn.silu(x)
def _sigmoid(x):
    return jax.nn.sigmoid(x)
def _layernorm(x, axis=-1, eps=1e-5):
    m = jnp.mean(x, axis=axis, keepdims=True)
    v = jnp.var(x, axis=axis, keepdims=True)
    return (x - m) / jnp.sqrt(v + eps)
def _scatter_add(tgt, idx, src, axis=0):
    return tgt.at[idx].add(src)
def _segment_sum(src, seg, n):
    return jax.ops.segment_sum(src, seg, n)

kernel_name = 'mk_conv_preact_d2_conv_nchw16_905872'

def setup_inputs(seed: int = 0):
    np.random.seed(seed)
    _w = jnp.asarray
    def _rec_inputs():
        import jax
        import jax.numpy as jnp
        _gk = jax.random.key(seed)
        x = -7.109e-05 + 0.9999 * jax.random.normal(jax.random.fold_in(_gk, 1), (16, 16, 512, 512), jnp.float32)
        return x
    x = _rec_inputs()
    def _L0_conv_setup():
        import jax, jax.numpy as jnp
        import numpy as np
        B, C_IN, H, W = (16, 16, 512, 512)
        C_OUT, KH, KW = (16, 3, 3)
        N_EXPERTS = 3
        key = jax.random.key(seed)
        k1, k2, k3, k4 = jax.random.split(key, 4)
        x = jax.random.normal(k1, (B, C_IN, H, W), dtype=jnp.float32)
        fan_in = C_IN * KH * KW
        bound = np.sqrt(6.0 / fan_in)
        w_experts = jax.random.uniform(k2, (N_EXPERTS, C_OUT, C_IN, KH, KW), minval=-bound, maxval=bound, dtype=jnp.float32)
        bias = jnp.zeros((C_OUT,), dtype=jnp.float32)
        fc_bound = 1.0 / np.sqrt(C_IN)
        fc_w = jax.random.uniform(k3, (N_EXPERTS, C_IN), minval=-fc_bound, maxval=fc_bound, dtype=jnp.float32)
        fc_b = jnp.zeros((N_EXPERTS,), dtype=jnp.float32)
        return {'x': x, 'w_experts': w_experts, 'bias': bias, 'fc_w': fc_w, 'fc_b': fc_b}
    _L0_conv_all = _L0_conv_setup()
    _L0_conv_in = {k: v for k, v in _L0_conv_all.items() if k in ('w_experts', 'bias', 'fc_w', 'fc_b', )}
    del _L0_conv_all

    def _L1_conv_setup():
        import jax, jax.numpy as jnp
        import numpy as np
        from jax import lax
        K = 3
        P = 1
        _CONV_PAD = K - 1 - P

        def _rconv(a, w):
            return lax.conv_general_dilated(a, w, window_strides=(1, 1), padding=[(_CONV_PAD, _CONV_PAD), (_CONV_PAD, _CONV_PAD)], dimension_numbers=('NCHW', 'OIHW', 'NCHW'))
        key = jax.random.key(seed)
        k1, k2, k3, k4, k5 = jax.random.split(key, 5)
        N, C_IN, C_OUT, H, W = (8, 16, 16, 512, 512)
        x = jax.random.normal(k1, (N, C_IN, H, W), dtype=jnp.float32)
        scale = 1.0 / np.sqrt(C_IN * K * K)
        w_real = jax.random.normal(k2, (C_IN, C_OUT, K, K), dtype=jnp.float32) * scale
        w_imag = jax.random.normal(k3, (C_IN, C_OUT, K, K), dtype=jnp.float32) * scale
        b_real = jax.random.normal(k4, (C_OUT,), dtype=jnp.float32) * scale
        b_imag = jax.random.normal(k5, (C_OUT,), dtype=jnp.float32) * scale
        return {'x': x, 'w_real': w_real, 'w_imag': w_imag, 'b_real': b_real, 'b_imag': b_imag}
    _L1_conv_all = _L1_conv_setup()
    _L1_conv_in = {k: v for k, v in _L1_conv_all.items() if k in ('w_real', 'w_imag', 'b_real', 'b_imag', )}
    del _L1_conv_all

    return {
        "x": x,
        "L0_conv_w_experts": _L0_conv_in["w_experts"],
        "L0_conv_bias": _L0_conv_in["bias"],
        "L0_conv_fc_w": _L0_conv_in["fc_w"],
        "L0_conv_fc_b": _L0_conv_in["fc_b"],
        "L1_conv_w_real": _L1_conv_in["w_real"],
        "L1_conv_w_imag": _L1_conv_in["w_imag"],
        "L1_conv_b_real": _L1_conv_in["b_real"],
        "L1_conv_b_imag": _L1_conv_in["b_imag"],
    }

def reference(x, L0_conv_w_experts, L0_conv_bias, L0_conv_fc_w, L0_conv_fc_b, L1_conv_w_real, L1_conv_w_imag, L1_conv_b_real, L1_conv_b_imag):
    import jax
    import jax.numpy as jnp
    def _L0_conv_ref(x, w_experts, bias, fc_w, fc_b):
        import jax, jax.numpy as jnp
        import numpy as np
        B, C_IN, H, W = (16, 16, 512, 512)
        C_OUT, KH, KW = (16, 3, 3)
        N_EXPERTS = 3
        pooled = x.mean(axis=(2, 3))
        routing = jax.nn.softmax(pooled @ fc_w.T + fc_b, axis=1)
        kernels = jnp.einsum('bn,noihw->boihw', routing, w_experts)
        xp = jnp.pad(x, ((0, 0), (0, 0), (1, 1), (1, 1)), mode='reflect')

        def conv_one(xi, ki):
            return jax.lax.conv_general_dilated(xi[None], ki, window_strides=(1, 1), padding='VALID', dimension_numbers=('NCHW', 'OIHW', 'NCHW'))[0]
        out = jax.vmap(conv_one)(xp, kernels)
        return out + bias[None, :, None, None]

    def _L1_conv_ref(x, w_real, w_imag, b_real, b_imag):
        import jax, jax.numpy as jnp
        import numpy as np
        from jax import lax
        K = 3
        P = 1
        _CONV_PAD = K - 1 - P

        def _rconv(a, w):
            return lax.conv_general_dilated(a, w, window_strides=(1, 1), padding=[(_CONV_PAD, _CONV_PAD), (_CONV_PAD, _CONV_PAD)], dimension_numbers=('NCHW', 'OIHW', 'NCHW'))
        X = jnp.fft.rfftn(x, axes=(-2, -1), norm='backward')
        Xr, Xi = (jnp.real(X), jnp.imag(X))
        wr = jnp.transpose(jnp.flip(w_real, axis=(-2, -1)), (1, 0, 2, 3))
        wi = jnp.transpose(jnp.flip(w_imag, axis=(-2, -1)), (1, 0, 2, 3))
        Yr = _rconv(Xr, wr) - _rconv(Xi, wi) + b_real[:, None, None]
        Yi = _rconv(Xr, wi) + _rconv(Xi, wr) + b_imag[:, None, None]
        Y = lax.complex(Yr, Yi)
        return jnp.fft.irfftn(Y, axes=(-2, -1), norm='backward')

    def _gn(v, G=8, eps=1e-5):
        B_, C_, H_, W_ = v.shape
        g = v.reshape(B_, G, C_ // G, H_, W_)
        m = jnp.mean(g, axis=(2, 3, 4), keepdims=True)
        s = jnp.var(g, axis=(2, 3, 4), keepdims=True)
        return ((g - m) / jnp.sqrt(s + eps)).reshape(v.shape)

    def _ln_c(v, eps=1e-6):
        m = jnp.mean(v, axis=1, keepdims=True)
        s = jnp.var(v, axis=1, keepdims=True)
        return (v - m) / jnp.sqrt(s + eps)

    def _ln_t(v, eps=1e-5):
        m = jnp.mean(v, axis=-1, keepdims=True)
        s = jnp.var(v, axis=-1, keepdims=True)
        return (v - m) / jnp.sqrt(s + eps)

    def _to_tokens(v):
        B_, C_, H_, W_ = v.shape
        return v.reshape(B_, C_, H_ * W_).transpose(0, 2, 1)
    def _from_tokens(t, like):
        B_, C_, H_, W_ = like.shape
        return t.transpose(0, 2, 1).reshape(B_, C_, H_, W_)

    x = x + _L0_conv_ref(_gn(x), L0_conv_w_experts, L0_conv_bias, L0_conv_fc_w, L0_conv_fc_b)
    x = x + _L1_conv_ref(_gn(x), L1_conv_w_real, L1_conv_w_imag, L1_conv_b_real, L1_conv_b_imag)
    return x


_drawn_inputs = setup_inputs


def setup_inputs(seed=0):
    import zlib

    import numpy as np

    out = dict(_drawn_inputs(seed))
    spreads = {'L0_conv_bias': (0.0, 0.1), 'L0_conv_fc_b': (0.0, 0.296)}
    factors = {'L0_conv_fc_w': 172.287, 'L1_conv_b_real': 200.0, 'L1_conv_b_imag': 200.0}
    for name, (base, spread) in spreads.items():
        noise = np.random.default_rng([zlib.crc32(name.encode()), seed]).standard_normal(out[name].shape)
        drawn = base * np.exp(spread * noise) if base else spread * noise
        out[name] = jnp.asarray(drawn.astype(out[name].dtype))
    for name, factor in factors.items():
        out[name] = (out[name] * factor).astype(out[name].dtype)
    return out
```

```python
from contextlib import ExitStack

import concourse.bass as bass
from concourse import mybir

ALU = mybir.AluOpType
ACT = mybir.ActivationFunctionType
F32 = mybir.dt.float32
AX_X = mybir.AxisListType.X

P = 128
C = 16
W = 512
D = 8
NS = W // D
HW2 = W // 2
UN = 4
IT = NS // UN
NX = 3
NF = 3 * C
XW = W + 2
HALO_W = W + 4
EPS = 1e-5

SEMS = """
waits_passed consts_loaded em_copied bases_built wj_built
left_edges edges_ready conv_done half_ready fold_done acc_zeroed acc0_done accc_done accs_done sq_done s_done sj_kept
stats_read x0_ready xcs_ready beta_done bt_ready wq_ready y_done yp_ready y_out_ready
g0_aggr g0_mean g0_mu g0_dev g0_q g0_qps g0_var g0_sd g0_rs g0_pm g0_pmb g0_lps g0_logit g0_max g0_nmax g0_exp g0_rsum
g0_route g0_scal g0_w0 g0_w1 g0_w2 g0_bps g0_bsub g0_b2 g0_conv_weights
g1_sum g1_m1 g1_ps g1_mu g1_dmu g1_dmu2 g1_var g1_sd g1_rs g1_k g1_scal g1_acc g1_rps g1_r g1_rt g1_srsum g1_srz g1_aps
g1_bt g1_jfs g1_jf g1_frows g1_jfc g1_jfsum g1_zmod g1_z1 g1_z2 g1_z3 g1_jps g1_jt g1_bj f_ready
""".split()


def emit(nc, x, e_main, e_halo, bias, fcw, fcb, d_all, gf_raw, em, frow, trig, hmat, modt, gavg, ghalo, ident, sel,
         sgn, out):
    B = x.shape[0]
    sdict = {}
    with ExitStack() as ctx:
        def sb(name, shape, dt=F32):
            return ctx.enter_context(nc.sbuf_tensor(name, shape, dt))

        def sem(name):
            return ctx.enter_context(nc.semaphore(name))

        for name in SEMS:
            sdict[name] = sem(name)
        s = sdict
        x_loaded = [sem(f"x_loaded{i}") for i in range(2)]
        halo_loaded = [sem(f"halo_loaded{i}") for i in range(2)]
        w_loaded = [sem(f"w_loaded{i}") for i in range(2)]
        w_stored = [sem(f"w_stored{i}") for i in range(2)]
        y_stored = [sem(f"y_stored{i}") for i in range(2)]

        x1 = sb("x1", [P, NS, 2, 2, P])
        emain = sb("emain", [P, NX, 3 * P])
        ehalo = sb("ehalo", [96, NX, P])
        wc = sb("wc", [P, 3, P])
        wh = sb("wh", [96, P])
        djt = sb("djt", [P, 2, 3, 2, P])
        tr = sb("tr", [P, 2, 2, P])
        hm = sb("hm", [P, 2, 2, P])
        mod = sb("mod", [P, 2, NS])
        g1m = sb("g1m", [P, P])
        ghm = sb("ghm", [P, 96])
        idm = sb("idm", [P, P])
        selm = sb("selm", [P, 3, NF])
        gfr = sb("gfr", [NF, 2, 3, NF])
        sgm = sb("sgm", [NF, 2, NF])
        fwt = sb("fwt", [NF, 6, NF])
        biast = sb("biast", [P, 1])
        fcwt = sb("fcwt", [P, NX])
        fcbt = sb("fcbt", [P, NX])
        acc = sb("acc", [P, 3, W])
        xt = sb("xt", [P, 2, 3, 2, 2, P])
        wring = sb("wring", [P, 2, 7, P])
        xs = sb("xs", [P, 2, 2, XW])
        halo = sb("halo", [P, 2, 2, HALO_W])
        hflat = halo[:].rearrange("k a b c -> k (a b c)")
        bt = hflat[:, 0:2 * W].rearrange("k (a b c d) -> k a b c d", a=2, b=2, c=2)
        yt = hflat[:, 2 * W:4 * W].rearrange("k (a b) -> k a b", a=2)
        tmph = sb("tmph", [P, 2, 2, P])
        junk = sb("junk", [P, 2, HW2], mybir.dt.bfloat16)
        junk2 = sb("junk2", [P, 4, P], mybir.dt.bfloat16)
        bst = sb("bst", [P, NS, 6])
        ssq = sb("ssq", [P, 2, NS])
        sj = sb("sj", [P, 4, NS])
        sjt = sb("sjt", [P, 4, UN])
        bj = sb("bj", [P, 2, NS])
        ft = sb("ft", [96, 2, 2, P])
        sm = sb("sm", [P, 48])
        small = sb("small", [P, 12, NX])
        onesm = sb("onesm", [P, P])
        pmb = sb("pmb", [P, P])
        dsig = sb("dsig", [P, P])

        zt = xt[:, 1].rearrange("k a b c d -> k (a b c d)")
        bases = x1[:, 0:5].rearrange("k a b c d -> k (a b c d)")[:, 0:18 * P].rearrange(
            "k (u t n) -> k u t n", u=3, t=6)
        dall = x1[:, 5:10].rearrange("k a b c d -> k (a b c d)")[:, 0:18 * P].rearrange(
            "k (r a e n) -> k r a e n", r=2, a=3, e=3)

        def col(i, n=P):
            return sm[0:n, i:i + 1]
        (MV0, MV1, MU0, DEV, Q0, SD0, RS0, PM, RSH, MUH, SDH, NMX, ESUM, RSUM, B2, NMU0, NB1, MU1, E1, DM, VAR1, SD1,
         RS1, KJ, M1, Q1, ACB, SUMA, VAR0, JFE, JFO, TMPB, HSIG, MXL) = range(34)
        SR = 36
        SZ = 40

        def ps(name):
            return ctx.enter_context(nc.psum_tensor(name, [P, W], F32))
        cps = [ps(f"cps{i}") for i in range(4)]
        pstat = ps("pstat")
        pf = ps("pf")
        pbf = ps("pbf")
        pj = ps("pj")

        scratch = nc.dram_tensor("wj_scratch", [NS, P, 7, P], F32, kind="Internal").ap()
        x5 = x.rearrange("b c (j d) n -> b j c d n", d=D)
        xh = x.rearrange("b c (j d) n -> b j d c n", d=D)
        o5 = out.rearrange("b c (j d) n -> b j c d n", d=D)

        const_dmas = [
            (emain[:], e_main), (ehalo[:], e_halo), (biast[:], bias), (fcwt[:], fcw), (fcbt[:], fcb),
            (dall, d_all), (djt[:, :, :, 0], d_all[:, :, :, 0]), (djt[:, :, :, 1], d_all[:, :, :, 2]),
            (gfr[:], gf_raw), (ft[:], frow), (tr[:], trig), (hm[:], hmat), (mod[:], modt), (g1m[:], gavg),
            (ghm[:], ghalo), (idm[:], ident), (selm[:], sel), (sgm[:], sgn)]
        CONSTS = 16 * len(const_dmas)

        def turns(eng, body, peel_first=False, peel_last=False):
            lo, hi = int(peel_first), IT - int(peel_last)
            if peel_first:
                body(0)
            with eng.Fori(lo, hi) as it:
                body(it)
            if peel_last:
                body(IT - 1)

        def settle(eng):
            eng.sem_inc(s["waits_passed"], 1)

        block = ctx.enter_context(nc.Block())

        @block.sync
        def _(sp):
            for dst, src in const_dmas:
                sp.dma_start(dst, src).then_inc(s["consts_loaded"], 16)
            sp.dma_start(scratch[:, :, 6, :], em).then_inc(s["em_copied"], 16)
            with sp.Fori(0, NS // 2) as h:
                for u in range(2):
                    sp.wait_ge(s["wj_built"], 2 * h + u + 1)
                    sp.dma_start(scratch[2 * h + u, :, 0:6, :], wring[:, u, 0:6, :]).then_inc(w_stored[u], 16)
            for u in range(2):
                sp.wait_ge(w_stored[u], 16 * (NS // 2) + 16)
            sp.wait_ge(s["em_copied"], 16)

            def load_stats_group(b, it, v):
                sp.wait_ge(s["stats_read"], b * NS + it * UN + 2 * v + 2)
                for w in range(2):
                    sp.dma_start(xs[:, v, w, 1:1 + W], x5[b, it * UN + 2 * v + w]).then_inc(x_loaded[v], 16)

            with sp.Fori(0, IT) as it:
                for v in range(2):
                    load_stats_group(0, it, v)

            def image(b, more):
                def conv_turn(it):
                    first, last = isinstance(it, int) and it == 0, isinstance(it, int) and it == IT - 1
                    for v in range(2):
                        j = it * UN + 2 * v
                        sp.wait_ge(s["stats_read"], b * NS + NS + 4)
                        settle(sp)
                        sp.wait_ge(s["conv_done"], b * NS + it * UN + 2 * v + 2)
                        settle(sp)
                        for w in range(2):
                            sp.dma_start(xs[:, v, w, 1:1 + W], x5[b, j + w]).then_inc(x_loaded[v], 16)
                        sp.wait_ge(s["y_done"], b * NS + 2)
                        for q in range(2):
                            sp.wait_ge(y_stored[q], b * (16 * NS // 2) + 16)
                        for t in range(3):
                            c0 = 3 - t
                            top = halo[32 * t:32 * t + C, v, :, c0:c0 + W]
                            bot = halo[32 * t + C:32 * t + 2 * C, v, :, c0:c0 + W]
                            if first and v == 0:
                                tsrc = xh[b, 0].rearrange("d c n -> c d n")[:, 1:8:6]
                            else:
                                tsrc = xh[b, bass.ds(j - 1, 2), D - 1].rearrange("j c n -> c j n")
                            if last and v == 1:
                                bsrc = xh[b, NS - 1].rearrange("d c n -> c d n")[:, 0:7:6]
                            else:
                                bsrc = xh[b, bass.ds(j + 1, 2), 0].rearrange("j c n -> c j n")
                            sp.dma_start(top, tsrc).then_inc(halo_loaded[v], 16)
                            sp.dma_start(bot, bsrc).then_inc(halo_loaded[v], 16)
                turns(sp, conv_turn, peel_first=True, peel_last=True)

                def store(b, i, slot, turn):
                    sp.wait_ge(s["y_out_ready"], b * NS + i + 1 + 2)
                    settle(sp)
                    sp.dma_start(o5[b, i], yt[:, slot]).then_inc(y_stored[slot], 16)

                def mix_turn(it):
                    for u in range(UN):
                        i = it * UN + u
                        if more and u % 2 == 0:
                            sp.wait_ge(s["conv_done"], b * NS + NS + 4)
                            settle(sp)
                            sp.wait_ge(s["stats_read"], b * NS + NS + it * UN + u + 2)
                            for w in range(2):
                                sp.dma_start(xs[:, u // 2, w, 1:1 + W], x5[b + 1, i + w]).then_inc(x_loaded[u // 2], 16)
                        sp.wait_ge(s["y_done"], b * NS + i + 1)
                        sp.dma_start(wring[:, u % 2], scratch[i]).then_inc(w_loaded[u % 2], 16)
                        if not (isinstance(it, int) and it == 0 and u == 0):
                            store(b, i - 1, (u + 1) % 2, it)
                turns(sp, mix_turn, peel_first=True)
                store(b, NS - 1, 1, IT)

            with sp.Fori(0, B - 1) as b:
                image(b, True)
            image(B - 1, False)
            for q in range(2):
                sp.wait_ge(y_stored[q], B * (16 * NS // 2) + 16)

        @block.gpsimd
        def _(pool):
            pool.wait_ge(s["consts_loaded"], CONSTS)
            nc.gpsimd.memset(onesm[:], 1.0).then_inc(s["bases_built"], 1)

            def image(b):
                pool.wait_ge(s["f_ready"], b + 1)
                settle(pool)
                nc.gpsimd.memset(acc[:], 0.0).then_inc(s["acc_zeroed"], 1)
                pool.wait_ge(s["acc_zeroed"], b + 1)

                def edges(it, v, g):
                    pool.wait_ge(x_loaded[v], (2 * b * IT + IT + it + 1) * 32)
                    pool.wait_ge(halo_loaded[v], (b * IT + it + 1) * 96)
                    settle(pool)
                    nc.gpsimd.tensor_copy(xs[:, v, :, 0:XW:XW - 1], xs[:, v, :, 2:W:W - 3])
                    nc.gpsimd.tensor_copy(halo[0:32, v, :, 2:3], halo[0:32, v, :, 4:5]).then_inc(s["left_edges"], 1)
                    pool.wait_ge(s["left_edges"], b * (NS // 2) + (g + 1))
                    settle(pool)
                    nc.gpsimd.tensor_copy(halo[64:96, v, :, W + 1:W + 2],
                                          halo[64:96, v, :, W - 1:W]).then_inc(s["edges_ready"], 1)
                    pool.wait_ge(s["edges_ready"], b * (NS // 2) + (g + 1))
                    settle(pool)

                edges(0, 0, 0)

                def turn(it):
                    last = isinstance(it, int)
                    for v in range(2):
                        if not (last and v == 1):
                            edges(it + v, 1 - v, it * 2 + v + 1)
                        for w in range(2):
                            i = it * UN + 2 * v + w
                            pool.wait_ge(s["fold_done"], b * NS + i + 5)
                            pool.wait_ge(s["acc0_done"], b * NS + i + 1)
                            nc.gpsimd.tensor_tensor(acc[:, 0], acc[:, 0], x1[:, i].rearrange("k a b c -> k (a b c)"),
                                                    ALU.add).then_inc(s["acc0_done"], 1)
                turns(pool, turn, peel_last=True)

                pool.wait_ge(s["g1_bj"], b + 1)
                settle(pool)

                def mix_turn(it):
                    for u in range(UN):
                        pool.wait_ge(w_loaded[u % 2], (b * (NS // 2) + it * 2 + u // 2 + 1) * 16)
                        nc.gpsimd.tensor_tensor(wring[:, u % 2, 0], wring[:, u % 2, 0], dsig[:],
                                                ALU.add).then_inc(s["wq_ready"], 1)
                turns(pool, mix_turn)

            with pool.Fori(0, B) as b:
                image(b)

        @block.tensor
        def _(pe):
            pe.wait_ge(s["consts_loaded"], CONSTS)
            pe.sem_inc(s["conv_done"], 4)
            pe.sem_inc(s["y_done"], 2)

            def image(b):
                pe.wait_ge(s["g0_aggr"], b + 1)
                nc.tensor.matmul(pstat[:, 0:1], g1m[:], col(MV0), start=True, stop=True)
                nc.tensor.matmul(pstat[0:96, 1:2], ghm[:], col(MV0), start=True, stop=True).then_inc(s["g0_mean"], 1)
                pe.wait_ge(s["g0_q"], b + 1)
                nc.tensor.matmul(pstat[:, 2:3], g1m[:], col(Q0), start=True, stop=True)
                nc.tensor.matmul(pstat[0:96, 3:4], ghm[:], col(Q0), start=True, stop=True).then_inc(s["g0_qps"], 1)
                pe.wait_ge(s["g0_pmb"], b + 1)
                nc.tensor.matmul(pstat[:, 4:4 + NX], pmb[:], fcwt[:], start=True, stop=True).then_inc(s["g0_lps"], 1)
                pe.wait_ge(s["g0_w2"], b + 1)
                for t in range(3):
                    nc.tensor.matmul(pstat[:, 8:9], wc[:, t], col(MU0), start=t == 0, stop=False)
                nc.tensor.matmul(pstat[:, 8:9], wh[:], col(MUH, 96), start=False, stop=True).then_inc(s["g0_bps"], 1)
                pe.wait_ge(s["g0_conv_weights"], b + 1)
                settle(pe)

                def conv_turn(it):
                    for u in range(UN):
                        k = b * NS + it * UN + u
                        if u % 2 == 0:
                            pe.wait_ge(s["edges_ready"], b * (NS // 2) + it * 2 + u // 2 + 1)
                        pe.wait_ge(s["fold_done"], k + 1)
                        for t in range(3):
                            nc.tensor.matmul(cps[u][:], wc[:, t], xs[:, u // 2, u % 2, t:t + W], start=t == 0, stop=False)
                        nc.tensor.matmul(cps[u][:], wh[:], halo[0:96, u // 2, u % 2, 2:2 + W],
                                         start=False, stop=True).then_inc(s["conv_done"], 1)
                turns(pe, conv_turn)

                pe.wait_ge(s["g1_m1"], b + 1)
                nc.tensor.matmul(pstat[:, 16:18], g1m[:], sm[:, M1:M1 + 2], start=True, stop=True).then_inc(s["g1_ps"], 1)
                pe.wait_ge(s["g1_acc"], b + 1)
                for t in range(3):
                    last = nc.tensor.matmul(pf[0:NF, :], selm[:, t], acc[:, t], start=t == 0, stop=t == 2)
                last.then_inc(s["g1_rps"], 1)
                pe.wait_ge(s["g1_z3"], b + 1)
                for e in range(2):
                    for a in range(3):
                        for r in range(2):
                            z = zt[:, ((e * 3 + a) * 2 + r) * NS:((e * 3 + a) * 2 + r + 1) * NS]
                            last = nc.tensor.matmul(pj[:, e * NS:(e + 1) * NS], djt[:, r, a, 1 - e], z,
                                                    start=(a, r) == (0, 0), stop=(a, r) == (2, 1))
                last.then_inc(s["g1_jps"], 1)
                pe.wait_ge(s["g1_rt"], b + 1)
                for sg in range(2):
                    for p in range(2):
                        for t in range(3):
                            last = nc.tensor.matmul(pbf[:, (2 * sg + p) * NF:(2 * sg + p + 1) * NF],
                                                    xt[0:NF, 0, t, sg, p], fwt[:, 3 + t], start=t == 0, stop=t == 2)
                last.then_inc(s["g1_aps"], 1)
                pe.wait_ge(s["g1_srz"], b + 1)
                settle(pe)
                for e in range(2):
                    nc.tensor.matmul(pstat[0:NF, 32 + e:33 + e], gfr[:, 0, 2 - 2 * e], col(SZ + 2 * e, NF), start=True,
                                     stop=False)
                    last = nc.tensor.matmul(pstat[0:NF, 32 + e:33 + e], gfr[:, 1, 2 - 2 * e], col(SZ + 2 * e + 1, NF),
                                            start=False, stop=True)
                last.then_inc(s["g1_jfs"], 1)
                for t in range(3):
                    nc.tensor.matmul(pf[0:NF, :], fwt[:, t], xt[0:NF, 0, t].rearrange("k a b c -> k (a b c)"),
                                     start=t == 0, stop=False)
                pe.wait_ge(s["g1_bt"], b + 1)
                for sg in range(2):
                    for p in range(2):
                        o = (2 * sg + 1 - p) * P
                        last = nc.tensor.matmul(pf[0:NF, o:o + P], bt[:, 0, sg, p, 0:NF], hm[:, sg, p], start=False,
                                                stop=(sg, p) == (1, 1))
                last.then_inc(s["g1_frows"], 1)
                pe.wait_ge(s["f_ready"], b + 2)
                settle(pe)

                def mix_turn(it):
                    for u in range(UN):
                        k = b * NS + it * UN + u
                        v = u % 2
                        pe.wait_ge(s["xcs_ready"], k + 1)
                        pe.wait_ge(w_loaded[v], (b * (NS // 2) + it * 2 + u // 2 + 1) * 16)
                        for sg in range(2):
                            for p in range(2):
                                for t in range(3):
                                    last = nc.tensor.matmul(cps[v][:, (2 * sg + p) * P:(2 * sg + p + 1) * P],
                                                            xt[:, v, t, sg, p], wring[:, v, 3 + t], start=t == 0,
                                                            stop=t == 2)
                        last.then_inc(s["beta_done"], 1)
                        pe.wait_ge(s["wq_ready"], k + 1)
                        pe.wait_ge(s["y_out_ready"], k + 1)
                        for t in range(3):
                            nc.tensor.matmul(cps[2 + v][:], wring[:, v, t], xt[:, v, t].rearrange("k a b c -> k (a b c)"),
                                             start=t == 0, stop=False)
                        nc.tensor.matmul(cps[2 + v][:], wring[0:96, v, 6], ft[:].rearrange("k a b c -> k (a b c)"),
                                         start=False, stop=False)
                        pe.wait_ge(s["bt_ready"], k + 1)
                        for sg in range(2):
                            for p in range(2):
                                o = (2 * sg + 1 - p) * P
                                last = nc.tensor.matmul(cps[2 + v][:, o:o + P], bt[:, v, sg, p], hm[:, sg, p],
                                                        start=False, stop=(sg, p) == (1, 1))
                        last.then_inc(s["y_done"], 1)
                turns(pe, mix_turn)

            with pe.Fori(0, B) as b:
                image(b)

        @block.scalar
        def _(act):
            act.sem_inc(s["f_ready"], 1)
            act.wait_ge(s["consts_loaded"], CONSTS)

            def image(b):
                act.wait_ge(s["g0_var"], b + 1)
                nc.scalar.activation(col(SD0), col(VAR0), ACT.Sqrt)
                nc.scalar.activation(col(SDH, 96), col(TMPB, 96), ACT.Sqrt).then_inc(s["g0_sd"], 1)
                act.wait_ge(s["g0_nmax"], b + 1)
                nc.scalar.activation(small[:, 2], small[:, 1], ACT.Exp, bias=col(NMX), accum_out=col(ESUM)).then_inc(
                    s["g0_exp"], 1)
                act.wait_ge(s["g0_b2"], b + 1)

                def square(k, i):
                    act.wait_ge(s["fold_done"], k + 5)
                    act.wait_ge(s["sq_done"], k + 1)
                    nc.scalar.activation(junk[:, 0], x1[:, i, 0].rearrange("k a b -> k (a b)"), ACT.Square, bias=col(NMU0),
                                         accum_out=ssq[:, 0, bass.ds(i, 1)])
                    nc.scalar.activation(junk[:, 1], x1[:, i, 1].rearrange("k a b -> k (a b)"), ACT.Square,
                                         accum_out=ssq[:, 1, bass.ds(i, 1)]).then_inc(s["sq_done"], 1)

                def conv_turn(it):
                    for u in range(UN):
                        i = it * UN + u
                        k = b * NS + i
                        act.wait_ge(s["conv_done"], k + 5)
                        act.wait_ge(s["fold_done"], k + 3)
                        nc.scalar.activation(tmph[:, u % 2].rearrange("k p t -> k t p"),
                                             cps[u][:, HW2:W].rearrange("k (t p) -> k t p", p=2),
                                             ACT.Copy).then_inc(s["half_ready"], 1)
                        if u:
                            square(k - 1, i - 1)
                    square(b * NS + it * UN + UN - 1, it * UN + UN - 1)
                turns(act, conv_turn)

                act.wait_ge(s["g1_var"], b + 1)
                nc.scalar.activation(col(SD1), col(VAR1), ACT.Sqrt).then_inc(s["g1_sd"], 1)
                act.wait_ge(s["g1_rps"], b + 1)
                nc.scalar.activation(xt[0:NF, 0, 0].rearrange("k a b c -> k (a b c)"), pf[0:NF, :],
                                     ACT.Copy).then_inc(s["g1_r"], 1)
                act.wait_ge(s["g1_aps"], b + 1)
                for sg in range(2):
                    for p in range(2):
                        last = nc.scalar.activation(bt[:, 0, sg, p, 0:NF],
                                                    pbf[:, (2 * sg + p) * NF:(2 * sg + p + 1) * NF], ACT.Copy)
                last.then_inc(s["g1_bt"], 1)
                act.wait_ge(s["g1_frows"], b + 1)
                act.wait_ge(s["g1_jf"], b + 1)
                for p in range(2):
                    nc.scalar.activation(ft[0:NF, 0, p], pf[0:NF, p * P:(p + 1) * P], ACT.Identity,
                                         bias=col(JFE + p, NF))
                nc.scalar.activation(ft[0:NF, 1].rearrange("k a b -> k (a b)"), pf[0:NF, HW2:W],
                                     ACT.Copy).then_inc(s["f_ready"], 1)
                act.wait_ge(s["g1_bj"], b + 1)

                def normalise(k, i, v):
                    act.wait_ge(s["y_done"], k + 1)
                    nc.scalar.activation(xt[:, v, 0, 0], x1[:, i, 0], ACT.Identity, scale=col(RS1), bias=col(NB1))
                    nc.scalar.activation(xt[:, v, 0, 1], x1[:, i, 1], ACT.Copy, scale=col(RS1)).then_inc(
                        s["x0_ready"], 1)

                normalise(b * NS, 0, 0)

                def mix_turn(it):
                    for u in range(UN):
                        i = it * UN + u
                        k = b * NS + i
                        v = u % 2
                        act.wait_ge(s["beta_done"], k + 1)
                        nc.scalar.activation(bt[:, v].rearrange("k a b c -> k (a b c)"), cps[v][:],
                                             ACT.Copy).then_inc(s["bt_ready"], 1)
                        if not (isinstance(it, int) and u == UN - 1):
                            normalise(k + 1, i + 1, 1 - v)
                        act.wait_ge(s["y_done"], k + 3)
                        act.wait_ge(s["y_out_ready"], k + 1)
                        for p in range(2):
                            last = nc.scalar.activation(tmph[:, v, p], cps[2 + v][:, p * P:(p + 1) * P], ACT.Identity,
                                                        bias=bj[:, p, bass.ds(i, 1)])
                        last.then_inc(s["yp_ready"], 1)
                turns(act, mix_turn, peel_last=True)

            with act.Fori(0, B) as b:
                image(b)

        @block.vector
        def _(dve):
            tt = nc.vector.tensor_tensor
            stt = nc.vector.scalar_tensor_tensor
            ts = nc.vector.tensor_scalar

            dve.sem_inc(s["stats_read"], 4)
            dve.sem_inc(s["fold_done"], 4)
            dve.sem_inc(s["y_out_ready"], 2)
            for name in ("s_done", "sq_done", "acc0_done", "accc_done", "accs_done", "sj_kept"):
                dve.sem_inc(s[name], 1)
            for free in (*w_stored, *y_stored):
                dve.sem_inc(free, 16)
            dve.wait_ge(s["consts_loaded"], CONSTS)

            def gr(u, e, sign):
                return {0: [(sign, 0, 1, e)], 1: [(sign, 0, 2, e), (sign, 0, 0, e)],
                        2: [(-sign, 1, 2, e), (sign, 1, 0, e)]}[u]

            def gi(u, e, sign):
                return {0: [(sign, 1, 1, e)], 1: [(sign, 1, 2, e), (sign, 1, 0, e)],
                        2: [(sign, 0, 2, e), (-sign, 0, 0, e)]}[u]

            built = 1
            dve.wait_ge(s["bases_built"], built)
            for u in range(3):
                types = [gr(u, 1, 1), gr(u, 2, 1) + gr(u, 0, 1), gi(u, 2, -1) + gi(u, 0, 1),
                         gi(u, 1, 1), gi(u, 2, 1) + gi(u, 0, 1), gr(u, 2, 1) + gr(u, 0, -1)]
                for t, terms in enumerate(types):
                    for n, (sign, r, a, e) in enumerate(terms):
                        if n == 0:
                            ins = ts(bases[:, u, t], dall[:, r, a, e], 0.5 * sign, None, ALU.mult)
                        else:
                            ins = stt(bases[:, u, t], dall[:, r, a, e], 0.5 * sign, bases[:, u, t], ALU.mult, ALU.add)
                        ins.then_inc(s["bases_built"], 1)
                        built += 1
                        dve.wait_ge(s["bases_built"], built)

            def strip_weights(j, h, u):
                dve.wait_ge(w_stored[u], 16 * h + 16)
                wv = wring[:, u, 0:6]
                stt(wv, bases[:, 1], mod[:, 0, bass.ds(j, 1)], bases[:, 0], ALU.mult, ALU.add).then_inc(
                    s["bases_built"], 1)
                dve.wait_ge(s["bases_built"], built + 1 + j)
                stt(wv, bases[:, 2], mod[:, 1, bass.ds(j, 1)], wv, ALU.mult, ALU.add).then_inc(s["wj_built"], 1)

            with dve.Fori(0, NS // 2) as h:
                for u in range(2):
                    strip_weights(2 * h + u, h, u)

            base = built + NS
            for r in range(2):
                for e in range(3):
                    tt(gfr[:, r, e], gfr[:, r, e], sgm[:, r], ALU.mult).then_inc(s["bases_built"], 1)
            dve.wait_ge(s["bases_built"], base + 6)
            nc.vector.tensor_copy(fwt[:, 0], gfr[:, 0, 1])
            tt(fwt[:, 1], gfr[:, 0, 2], gfr[:, 0, 0], ALU.add)
            tt(fwt[:, 2], gfr[:, 1, 0], gfr[:, 1, 2], ALU.subtract)
            nc.vector.tensor_copy(fwt[:, 3], gfr[:, 1, 1])
            tt(fwt[:, 4], gfr[:, 1, 2], gfr[:, 1, 0], ALU.add)
            tt(fwt[:, 5], gfr[:, 0, 2], gfr[:, 0, 0], ALU.subtract)

            def stats(i, v, w, count, k):
                if w == 0:
                    dve.wait_ge(x_loaded[v], count * 32)
                nc.vector.bn_stats(bst[:, i], xs[:, v, w, 1:1 + W]).then_inc(s["stats_read"], 1)

            with dve.Fori(0, IT) as it:
                for u in range(UN):
                    stats(it * UN + u, u // 2, u % 2, it + 1, 0)

            def image(b, more):
                n = b + 1
                dve.wait_ge(s["stats_read"], b * NS + NS + 4)
                settle(dve)
                nc.vector.bn_aggr(sm[:, MV0:MV0 + 2], bst[:].rearrange("k a b -> k (a b)")).then_inc(s["g0_aggr"], 1)
                dve.wait_ge(s["g0_mean"], n)
                nc.vector.tensor_copy(col(MU0), pstat[:, 0:1])
                nc.vector.tensor_copy(col(MUH, 96), pstat[0:96, 1:2]).then_inc(s["g0_mu"], 1)
                dve.wait_ge(s["g0_mu"], n)
                tt(col(DEV), col(MV0), col(MU0), ALU.subtract)
                ts(col(NMU0), col(MU0), -2.0, None, ALU.mult).then_inc(s["g0_dev"], 1)
                dve.wait_ge(s["g0_dev"], n)
                stt(col(Q0), col(DEV), col(DEV), col(MV1), ALU.mult, ALU.add).then_inc(s["g0_q"], 1)
                dve.wait_ge(s["g0_qps"], n)
                ts(col(VAR0), pstat[:, 2:3], EPS, None, ALU.add)
                ts(col(TMPB, 96), pstat[0:96, 3:4], EPS, None, ALU.add).then_inc(s["g0_var"], 1)
                dve.wait_ge(s["g0_sd"], n)
                nc.vector.reciprocal(col(RS0), col(SD0))
                nc.vector.reciprocal(col(RSH, 96), col(SDH, 96)).then_inc(s["g0_rs"], 1)
                dve.wait_ge(s["g0_rs"], n)
                ts(col(PM), col(DEV), col(RS0), 1.0 / D, ALU.mult, ALU.mult).then_inc(s["g0_pm"], 1)
                dve.wait_ge(s["g0_pm"], n)
                ts(pmb[:], onesm[:], col(PM), None, ALU.mult).then_inc(s["g0_pmb"], 1)
                dve.wait_ge(s["g0_lps"], n)
                tt(small[:, 1], pstat[:, 4:4 + NX], fcbt[:], ALU.add).then_inc(s["g0_logit"], 1)
                dve.wait_ge(s["g0_logit"], n)
                nc.vector.reduce_max(col(MXL), small[:, 1], AX_X).then_inc(s["g0_max"], 1)
                dve.wait_ge(s["g0_max"], n)
                ts(col(NMX), col(MXL), -1.0, None, ALU.mult).then_inc(s["g0_nmax"], 1)
                dve.wait_ge(s["g0_exp"], n)
                nc.vector.reciprocal(col(RSUM), col(ESUM)).then_inc(s["g0_rsum"], 1)
                dve.wait_ge(s["g0_rsum"], n)
                ts(small[:, 3], small[:, 2], col(RSUM), None, ALU.mult).then_inc(s["g0_route"], 1)
                dve.wait_ge(s["g0_route"], n)
                ts(small[:, 4], small[:, 3], col(RS0), None, ALU.mult)
                ts(small[0:96, 5], small[0:96, 3], col(RSH, 96), None, ALU.mult).then_inc(s["g0_scal"], 1)
                dve.wait_ge(s["g0_scal"], n)
                wcf = wc[:].rearrange("k a b -> k (a b)")
                ts(wcf, emain[:, 0], small[:, 4, 0:1], None, ALU.mult)
                ts(wh[:], ehalo[:, 0], small[0:96, 5, 0:1], None, ALU.mult).then_inc(s["g0_w0"], 1)
                dve.wait_ge(s["g0_w0"], n)
                stt(wcf, emain[:, 1], small[:, 4, 1:2], wcf, ALU.mult, ALU.add)
                stt(wh[:], ehalo[:, 1], small[0:96, 5, 1:2], wh[:], ALU.mult, ALU.add).then_inc(s["g0_w1"], 1)
                dve.wait_ge(s["g0_w1"], n)
                stt(wcf, emain[:, 2], small[:, 4, 2:3], wcf, ALU.mult, ALU.add)
                stt(wh[:], ehalo[:, 2], small[0:96, 5, 2:3], wh[:], ALU.mult, ALU.add).then_inc(s["g0_w2"], 1)
                dve.wait_ge(s["g0_bps"], n)
                tt(wc[:, 1], wc[:, 1], idm[:], ALU.add).then_inc(s["g0_conv_weights"], 1)
                tt(col(B2), biast[:], pstat[:, 8:9], ALU.subtract).then_inc(s["g0_bsub"], 1)
                dve.wait_ge(s["g0_bsub"], n)
                ts(col(B2), col(B2), 2.0, None, ALU.mult).then_inc(s["g0_b2"], 1)
                dve.wait_ge(s["g0_b2"], n)
                dve.wait_ge(s["acc_zeroed"], n)
                settle(dve)

                def conv_turn(it):
                    for u in range(UN):
                        i = it * UN + u
                        k = b * NS + i
                        first = cps[u][:, 0:HW2].rearrange("k (t p) -> k p t", p=2)
                        second = tmph[:, u % 2]
                        dve.wait_ge(s["half_ready"], k + 1)
                        stt(x1[:, i, 0], first, col(B2), second, ALU.add, ALU.add)
                        tt(x1[:, i, 1], first, second, ALU.subtract).then_inc(s["fold_done"], 1)
                        dve.wait_ge(s["fold_done"], k + 5)
                        xf = x1[:, i].rearrange("k a b c -> k (a b c)")
                        dve.wait_ge(s["accc_done"], k + 1)
                        stt(acc[:, 1], xf, mod[:, 0, bass.ds(i, 1)], acc[:, 1], ALU.mult, ALU.add).then_inc(
                            s["accc_done"], 1)
                        dve.wait_ge(s["accs_done"], k + 1)
                        stt(acc[:, 2], xf, mod[:, 1, bass.ds(i, 1)], acc[:, 2], ALU.mult, ALU.add).then_inc(
                            s["accs_done"], 1)
                        dve.wait_ge(s["s_done"], k + 1)
                        if u == 0:
                            dve.wait_ge(s["sj_kept"], b * IT + it + 1)
                        for t in range(2):
                            for p in range(2):
                                last = stt(junk2[:, 2 * t + p], x1[:, i, 1, p], 1.0, tr[:, t, p], ALU.mult, ALU.mult,
                                           accum_out=sjt[:, 2 * t + p, u:u + 1])
                        last.then_inc(s["s_done"], 1)
                    dve.wait_ge(s["s_done"], b * NS + it * UN + UN + 1)
                    nc.vector.tensor_copy(sj[:, :, bass.ds(it * UN, UN)], sjt[:]).then_inc(s["sj_kept"], 1)
                turns(dve, conv_turn)

                dve.wait_ge(s["acc0_done"], b * NS + NS + 1)
                dve.wait_ge(s["accc_done"], b * NS + NS + 1)
                dve.wait_ge(s["accs_done"], b * NS + NS + 1)
                dve.wait_ge(s["sj_kept"], b * IT + IT + 1)
                dve.wait_ge(s["sq_done"], b * NS + NS + 1)
                nc.vector.reduce_sum(col(SUMA), acc[:, 0, 0:HW2], AX_X)
                nc.vector.reduce_sum(col(DM), ssq[:].rearrange("k a b -> k (a b)"), AX_X).then_inc(s["g1_sum"], 1)
                dve.wait_ge(s["g1_sum"], n)
                ts(col(M1), col(SUMA), 1.0 / (NS * W), None, ALU.mult)
                ts(col(Q1), col(DM), 0.5 / (NS * W), None, ALU.mult).then_inc(s["g1_m1"], 1)
                dve.wait_ge(s["g1_ps"], n)
                nc.vector.tensor_copy(sm[:, MU1:MU1 + 2], pstat[:, 16:18]).then_inc(s["g1_mu"], 1)
                dve.wait_ge(s["g1_mu"], n)
                tt(col(DM), col(MU1), col(MU0), ALU.subtract).then_inc(s["g1_dmu"], 1)
                dve.wait_ge(s["g1_dmu"], n)
                tt(col(DM), col(DM), col(DM), ALU.mult).then_inc(s["g1_dmu2"], 1)
                dve.wait_ge(s["g1_dmu2"], n)
                ts(col(VAR1), col(E1), col(DM), EPS, ALU.subtract, ALU.add).then_inc(s["g1_var"], 1)
                dve.wait_ge(s["g1_sd"], n)
                nc.vector.reciprocal(col(RS1), col(SD1)).then_inc(s["g1_rs"], 1)
                dve.wait_ge(s["g1_rs"], n)
                tt(col(NB1), col(MU1), col(RS1), ALU.mult)
                ts(dsig[:], idm[:], col(SD1), 0.5, ALU.mult, ALU.mult)
                ts(col(KJ), col(RS1), -1.0 / W, None, ALU.mult).then_inc(s["g1_k"], 1)
                dve.wait_ge(s["g1_k"], n)
                ts(col(ACB), col(NB1), -2.0 * NS, None, ALU.mult).then_inc(s["g1_scal"], 1)
                dve.wait_ge(s["g1_scal"], n)
                ts(col(NB1), col(NB1), -2.0, None, ALU.mult)
                ts(acc[:, 0, 0:HW2], acc[:, 0, 0:HW2], col(RS1), col(ACB), ALU.mult, ALU.add)
                ts(acc[:, 0, HW2:W], acc[:, 0, HW2:W], col(RS1), None, ALU.mult)
                accf = acc[:, 1:3].rearrange("k a b -> k (a b)")
                ts(accf, accf, col(RS1), None, ALU.mult).then_inc(s["g1_acc"], 1)

                sjf = sj[:].rearrange("k (t p) j -> k t p j", p=2)
                q = zt[:, 12 * NS:24 * NS].rearrange("k (a j) -> k a j", j=NS)
                z = zt[:, 0:12 * NS].rearrange("k (e a r j) -> k e a r j", e=2, a=3, r=2)
                for t in range(2):
                    stt(q[:, t], sjf[:, t, 0], 1.0, sjf[:, t, 1], ALU.mult, ALU.add)
                    last = stt(q[:, 2 + t], sjf[:, t, 0], 1.0, sjf[:, t, 1], ALU.mult, ALU.subtract)
                last.then_inc(s["g1_z1"], 1)
                dve.wait_ge(s["g1_z1"], n)
                for e in range(2):
                    ts(z[:, e, 1, 0], q[:, 2 * e], col(KJ), None, ALU.mult)
                    last = ts(z[:, e, 1, 1], q[:, 2 * e + 1], col(KJ), (-1.0, 1.0)[e], ALU.mult, ALU.mult)
                last.then_inc(s["g1_z2"], 1)
                dve.wait_ge(s["g1_z2"], n)
                for e in range(2):
                    for r in range(2):
                        for t in range(2):
                            last = tt(q[:, 4 + 4 * e + 2 * r + t], z[:, e, 1, r], mod[:, t], ALU.mult)
                last.then_inc(s["g1_zmod"], 1)
                dve.wait_ge(s["g1_zmod"], n)
                for e in range(2):
                    cr, sr, ci, si = (q[:, 4 + 4 * e + t] for t in range(4))
                    tt(z[:, e, 2, 0], cr, si, ALU.add)
                    tt(z[:, e, 2, 1], ci, sr, ALU.subtract)
                    tt(z[:, e, 0, 0], cr, si, ALU.subtract)
                    last = tt(z[:, e, 0, 1], ci, sr, ALU.add)
                last.then_inc(s["g1_z3"], 1)

                dve.wait_ge(s["g1_r"], n)
                for t in range(2):
                    for p in range(2):
                        nc.vector.tensor_tensor_reduce(
                            out=xt[0:NF, 0, 1 + t, 0, p], in0=xt[0:NF, 0, 0, 1, p], in1=tr[0:NF, t, p], scale=1.0,
                            scalar=0.0, op0=ALU.mult, op1=ALU.add, accum_out=col(SR + 2 * t + p, NF))
                    last = tt(xt[0:NF, 0, 1 + t, 1], xt[0:NF, 0, 0, 0], tr[0:NF, t], ALU.mult)
                last.then_inc(s["g1_rt"], 1)
                dve.wait_ge(s["g1_rt"], n)
                for e in range(2):
                    op = (ALU.add, ALU.subtract)[e]
                    stt(col(SZ + 2 * e, NF), col(SR, NF), 1.0, col(SR + 1, NF), ALU.mult, op)
                stt(col(SZ + 3, NF), col(SR + 2, NF), 1.0, col(SR + 3, NF), ALU.mult, ALU.subtract)
                stt(col(SZ + 1, NF), col(SR + 2, NF), 1.0, col(SR + 3, NF), ALU.mult, ALU.add).then_inc(
                    s["g1_srsum"], 1)
                dve.wait_ge(s["g1_srsum"], n)
                ts(col(SZ + 1, NF), col(SZ + 1, NF), -1.0, None, ALU.mult).then_inc(s["g1_srz"], 1)
                dve.wait_ge(s["g1_jps"], n)
                ts(q[:, 0], pj[:, 0:NS], col(MU1), None, ALU.add).then_inc(s["g1_jt"], 1)
                dve.wait_ge(s["g1_jt"], n)
                tt(bj[:, 0], pj[:, NS:2 * NS], q[:, 0], ALU.add)
                stt(bj[:, 1], pj[:, NS:2 * NS], -1.0, q[:, 0], ALU.mult, ALU.add).then_inc(s["g1_bj"], 1)
                dve.wait_ge(s["g1_jfs"], n)
                nc.vector.tensor_copy(sm[0:NF, SR:SR + 2], pstat[0:NF, 32:34]).then_inc(s["g1_jfc"], 1)
                dve.wait_ge(s["g1_jfc"], n)
                stt(col(JFE, NF), col(SR, NF), 1.0, col(SR + 1, NF), ALU.mult, ALU.add)
                stt(col(JFO, NF), col(SR, NF), 1.0, col(SR + 1, NF), ALU.mult, ALU.subtract).then_inc(s["g1_jfsum"], 1)
                dve.wait_ge(s["g1_jfsum"], n)
                ts(sm[0:NF, JFE:JFE + 2], sm[0:NF, JFE:JFE + 2], -2.0 / W, None, ALU.mult).then_inc(s["g1_jf"], 1)

                def modulate(k, v):
                    dve.wait_ge(s["x0_ready"], k + 1)
                    for t in range(2):
                        tt(xt[:, v, 1 + t, 0], xt[:, v, 0, 1], tr[:, t], ALU.mult)
                        last = tt(xt[:, v, 1 + t, 1], xt[:, v, 0, 0], tr[:, t], ALU.mult)
                    last.then_inc(s["xcs_ready"], 1)

                modulate(b * NS, 0)

                def mix_turn(it):
                    for u in range(UN):
                        i = it * UN + u
                        k = b * NS + i
                        v = u % 2
                        if not (isinstance(it, int) and u == UN - 1):
                            modulate(k + 1, 1 - v)
                        if more:
                            stats(i, u // 2, u % 2, 2 * b * IT + 2 * IT + it + 1, k)
                        dve.wait_ge(s["yp_ready"], k + 1)
                        dve.wait_ge(y_stored[v], (b * (NS // 2) + it * 2 + u // 2 + 1) * 16)
                        yv = yt[:, v].rearrange("k (q t p) -> k q p t", q=2, p=2)
                        diff = cps[2 + v][:, HW2:W].rearrange("k (p t) -> k p t", p=2)
                        tt(yv[:, 0], diff, tmph[:, v], ALU.add)
                        tt(yv[:, 1], tmph[:, v], diff, ALU.subtract).then_inc(s["y_out_ready"], 1)
                turns(dve, mix_turn, peel_last=True)

            with dve.Fori(0, B - 1) as b:
                image(b, True)
            image(B - 1, False)


def kernel(x, L0_conv_w_experts, L0_conv_bias, L0_conv_fc_w, L0_conv_fc_b, L1_conv_w_real, L1_conv_w_imag,
           L1_conv_b_real, L1_conv_b_imag):
    import numpy as np
    import concourse.bacc as bacc
    from concourse.bass_utils import run_bass_kernel_spmd

    f32 = np.float32
    x = np.ascontiguousarray(x)
    we, wr, wi = (np.asarray(a) for a in (L0_conv_w_experts, L1_conv_w_real, L1_conv_w_imag))
    a = {"x": x}

    em = np.zeros((C, D, NX, 3, C, D), f32)
    eh = np.zeros((3, 2, C, NX, C, D), f32)
    for t in range(3):
        for d_in in range(D):
            for d_out in range(D):
                if 0 <= d_in - d_out + 1 <= 2:
                    em[:, d_in, :, t, :, d_out] = we[:, :, :, d_in - d_out + 1, t].transpose(2, 0, 1)
        eh[t, 0, :, :, :, 0] = we[:, :, :, 0, t].transpose(2, 0, 1)
        eh[t, 1, :, :, :, D - 1] = we[:, :, :, 2, t].transpose(2, 0, 1)
    a["e_main"] = em.reshape(P, NX, 3 * P)
    a["e_halo"] = eh.reshape(96, NX, P)
    a["bias"] = np.repeat(np.asarray(L0_conv_bias), D).reshape(P, 1)
    a["fcw"] = np.repeat(np.asarray(L0_conv_fc_w).T, D, axis=0).copy()
    a["fcb"] = np.tile(np.asarray(L0_conv_fc_b).reshape(1, NX), (P, 1))

    da = np.zeros((C, D, 2, 3, 3, C, D), f32)
    for r, w in enumerate((wr, wi)):
        for d in range(D):
            da[:, d, r, :, :, :, d] = w.transpose(0, 2, 3, 1)
    a["d_all"] = da.reshape(P, 2, 3, 3, P)

    gf = np.zeros((3, C, 2, 3, 3, C), f32)
    sg = np.zeros((3, C, 2, 3, C), f32)
    parts = (wr, wi)
    for r in range(2):
        for t, f, part, tap, sign in ((1, 0, r, 2, 1), (2, 0, 1 - r, 2, (-1, 1)[r]), (0, 1, r, 0, 1),
                                      (0, 2, 1 - r, 0, (1, -1)[r])):
            gf[t, :, r, :, f, :] = parts[part][:, :, tap, :].transpose(0, 2, 1)
            sg[t, :, r, f, :] = sign * (-0.5 / W)
    a["gf_raw"] = gf.reshape(NF, 2, 3, NF)
    a["sgn"] = sg.reshape(NF, 2, NF)

    theta = 2 * np.pi / W
    rows = theta * np.arange(W).reshape(NS, D)
    pl = np.zeros((NS, 128, C, D), f32)
    for o in range(C):
        pl[:, o, o] = 1.0
        pl[:, C + o, o] = np.cos(rows)
        pl[:, 2 * C + o, o] = np.sin(rows)
        pl[0, 64 + o, o, 0] = np.asarray(L1_conv_b_real)[o]
        pl[0, 80 + o, o, 0] = np.asarray(L1_conv_b_imag)[o]
    a["em"] = pl.reshape(NS, P, P)

    def hilbert(d):
        d = np.asarray(d)
        out = np.zeros(d.shape)
        odd = d % 2 != 0
        out[odd] = (2.0 / W) / np.tan(np.pi * d[odd] / W)
        return out

    n = 2 * np.arange(128)[None, :] + np.arange(2)[:, None]
    fr = np.zeros((96, 2, 2, P), f32)
    fr[64:80, :, 0, 0] = 0.5
    fr[80:96, 0] = -0.5 * (hilbert(n) + hilbert(n + HW2))
    fr[80:96, 1] = -0.5 * (hilbert(n) - hilbert(n + HW2))
    a["frow"] = fr
    a["trig"] = np.broadcast_to(np.stack([np.cos(theta * n), np.sin(theta * n)]).astype(f32), (P, 2, 2, P)).copy()
    hmat = np.zeros((P, 2, 2, P), f32)
    half = np.arange(P)
    for p in range(2):
        d = 2 * (half[None, :] - half[:, None]) + (1 - p) - p
        hmat[:, 0, p] = -(hilbert(d) + hilbert(d + HW2))
        hmat[:, 1, p] = -(hilbert(d) - hilbert(d + HW2))
    a["hmat"] = hmat
    md = np.stack([np.cos(rows.T), np.sin(rows.T)], 1).astype(f32)
    a["modt"] = np.tile(md, (C, 1, 1))
    grp = np.arange(P) // (2 * D)
    a["gavg"] = ((grp[:, None] == grp[None, :]) / (2.0 * D)).astype(f32)
    hgrp = (np.arange(96) % C) // 2
    a["ghalo"] = ((grp[:, None] == hgrp[None, :]) / (2.0 * D)).astype(f32)
    a["ident"] = np.eye(P, dtype=f32)
    sel = np.zeros((C, D, 3, 3, C), f32)
    for t in range(3):
        for c in range(C):
            sel[c, :, t, t, c] = 1.0
    a["sel"] = sel.reshape(P, 3, NF)

    nc = bacc.Bacc("TRN2", target_bir_lowering=False, num_devices=1)
    aps = {k: nc.dram_tensor(f"in_{k}", v.shape, F32, kind="ExternalInput").ap() for k, v in a.items()}
    out = nc.dram_tensor("out", x.shape, F32, kind="ExternalOutput").ap()
    emit(nc, out=out, **aps)
    r = run_bass_kernel_spmd(nc, [{f"in_{k}": v for k, v in a.items()}], core_ids=[0])
    return r.results[0]["out"]
```

```python
from contextlib import ExitStack

import concourse.bass as bass
from concourse import mybir

ALU = mybir.AluOpType
ACT = mybir.ActivationFunctionType
F32 = mybir.dt.float32
F16 = mybir.dt.float16
AX_X = mybir.AxisListType.X

P = 128
C = 16
W = 512
D = 8
NS = W // D
HW2 = W // 2
UN = 4
IT = NS // UN
NX = 3
NF = 3 * C
XW = W + 2
HALO_W = W + 4
EPS = 1e-5
WJ = 6 * P + P // 2
SX = 64.0
SW = 256.0
SB = 16.0
SY = SX * SW
SF = 64.0
SH = SY / SB
PAIRS = ((0, 0), (0, 1), (1, 0))

SEMS = """
bias_added bterm_mm g1_fh g1_fl g1_fm waits_passed consts_loaded em_copied bases_built wj_built
left_edges edges_ready conv_done half_ready fold_done acc_zeroed acc0_done accc_done accs_done sq_done s_done sj_kept
stats_read x0f_ready x0h_ready xcf_ready xsf_ready xch_ready xsh_ready x_ready beta_done bth_ready bt_ready y_done
yp_ready yr_ready y_out_ready wf_ready wh_ready
g0_aggr g0_mean g0_mu g0_dev g0_q g0_qps g0_var g0_sd g0_rs g0_pm g0_pmb g0_lps g0_logit g0_max g0_nmax g0_exp g0_rsum
g0_route g0_scal g0_w0 g0_w1 g0_w2 g0_bps g0_b2 g0_conv_weights
g1_sum g1_m1 g1_ps g1_mu g1_dmu g1_dmu2 g1_var g1_sd g1_rs g1_k g1_scal g1_acc g1_rps g1_r g1_rt g1_srsum g1_srz g1_aps
g1_bt g1_jfs g1_jf g1_frows g1_jfc g1_jfsum g1_zmod g1_z1 g1_z2 g1_z3 g1_jps g1_jt g1_bj f_ready
""".split()


def emit(nc, x, e_main, e_halo, bias, fcw, fcb, d_all, gf_raw, em, frow, trig, hmat, hmat16, modt, gavg, ghalo, ident, sel,
         sgn, fselt, brow_w, out):
    B = x.shape[0]
    sdict = {}
    with ExitStack() as ctx:
        def sb(name, shape, dt=F32):
            return ctx.enter_context(nc.sbuf_tensor(name, shape, dt))

        def sem(name):
            return ctx.enter_context(nc.semaphore(name))

        for name in SEMS:
            sdict[name] = sem(name)
        s = sdict
        x_loaded = [[sem(f"x_loaded{v}{w}") for w in range(2)] for v in range(2)]
        halo_loaded = [sem(f"halo_loaded{i}") for i in range(2)]
        w_loaded = [sem(f"w_loaded{i}") for i in range(2)]
        w_stored = [sem(f"w_stored{i}") for i in range(2)]
        y_stored = [sem(f"y_stored{i}") for i in range(2)]

        x1 = sb("x1", [P, NS, 2, 2, P])
        emain = sb("emain", [P, NX, 3 * P])
        ehalo = sb("ehalo", [96, NX, P])
        wc = sb("wc", [P, 3, P])
        wh = sb("wh", [96, P])
        djt = sb("djt", [P, 2, 3, 2, P])
        tr = sb("tr", [P, 2, 2, P])
        hm = sb("hm", [P, 2, 2, P])
        h16 = sb("h16", [P, 2, 2, 2, P], F16)
        mod = sb("mod", [P, 2, NS])
        g1m = sb("g1m", [P, P])
        ghm = sb("ghm", [P, 96])
        idm = sb("idm", [P, P])
        selm = sb("selm", [P, 3, NF])
        gfr = sb("gfr", [NF, 2, 3, P])
        sgm = x1[0:NF, 16, 0]
        fwt = sb("fwt", [NF, 6, P])
        biast = sb("biast", [P, 1])
        fcwt = sb("fcwt", [P, NX])
        fcbt = sb("fcbt", [P, NX])
        acc = sb("acc", [P, 3, W])
        xparts = sb("xparts", [P, 2, 3, W])
        x16 = xparts[:].bitcast(F16).rearrange("k v t (h a b c) -> k v t h a b c", h=2, a=2, b=2)
        wring = sb("wring", [P, 2, 7, P])
        wflat = wring[:].rearrange("k v t n -> k v (t n)")
        w16 = wring[:].bitcast(F16).rearrange("k v t (h n) -> k v t h n", h=2)
        xs = sb("xs", [P, 2, 2, XW])
        halo = sb("halo", [P, 2, 2, HALO_W])
        hflat = halo[:].rearrange("k a b c -> k (a b c)")
        b16 = hflat[:, 0:2 * W].bitcast(F16).rearrange("k (v h a b c) -> k v h a b c", v=2, h=2, a=2, b=2)
        yt = hflat[:, 2 * W:4 * W].rearrange("k (a b) -> k a b", a=2)
        btf = yt[:, 0].rearrange("k (a b c) -> k a b c", a=2, b=2)
        xf = acc[:].rearrange("k t (a b c) -> k t a b c", a=2, b=2)
        yp = sb("yp", [P, 2, 2, 2, P])
        tmph = yp[:, :, 0]
        junk = sb("junk", [P, 2, HW2], mybir.dt.bfloat16)
        junk2 = sb("junk2", [P, 4, P], mybir.dt.bfloat16)
        bst = sb("bst", [P, NS, 6])
        ssq = sb("ssq", [P, 2, NS])
        sj = sb("sj", [P, 4, NS])
        sjt = sb("sjt", [P, 4, UN])
        bj = sb("bj", [P, 2, NS])
        f16 = sb("f16", [P, 2, 2, P], F16)
        fsel = sb("fsel", [P, 2])
        bterm = sb("bterm", [P, 2, 2, P])
        ffull, fhigh, flow = yp[:, 0], yt[:, 1].rearrange("k (a b c) -> k a b c", a=2, b=2), yp[:, 1]
        sm = sb("sm", [P, 48])
        small = sb("small", [P, 12, NX])
        onesm = sb("onesm", [P, P])
        pmb = sb("pmb", [P, P])

        zt = xparts[:, 1].rearrange("k a b -> k (a b)")
        bases = x1[:, 0:5].rearrange("k a b c d -> k (a b c d)")[:, 0:18 * P].rearrange(
            "k (u t n) -> k u t n", u=3, t=6)
        dall = x1[:, 5:10].rearrange("k a b c d -> k (a b c d)")[:, 0:18 * P].rearrange(
            "k (r a e n) -> k r a e n", r=2, a=3, e=3)

        wf = x1[:, 10:14].rearrange("k a b c d -> k (a b c d)")[:, 0:12 * P].rearrange(
            "k (v t n) -> k v t n", v=2, t=6)

        bdiag, brow = x1[0:32, 14, 0, 0], x1[0:32, 15]

        def col(i, n=P):
            return sm[0:n, i:i + 1]
        (MV0, MV1, MU0, DEV, Q0, SD0, RS0, PM, RSH, MUH, SDH, NMX, ESUM, RSUM, B2, NMU0, NB1, MU1, E1, DM, VAR1, SD1,
         RS1, KJ, M1, Q1, ACB, SUMA, VAR0, JFE, JFO, TMPB, RSX, MXL) = range(34)
        SR = 36
        SZ = 40

        def ps(name):
            return ctx.enter_context(nc.psum_tensor(name, [P, W], F32))
        cps = [ps(f"cps{i}") for i in range(4)]
        pstat = ps("pstat")
        pf = ps("pf")
        pbf = ps("pbf")
        pj = ps("pj")

        scratch = nc.dram_tensor("wj_scratch", [NS, P, WJ], F32, kind="Internal").ap()
        x5 = x.rearrange("b c (j d) n -> b j c d n", d=D)
        xh = x.rearrange("b c (j d) n -> b j d c n", d=D)
        o5 = out.rearrange("b c (j d) n -> b j c d n", d=D)

        const_dmas = [
            (emain[:], e_main), (ehalo[:], e_halo), (biast[:], bias), (fcwt[:], fcw), (fcbt[:], fcb),
            (dall, d_all), (djt[:, :, :, 0], d_all[:, :, :, 0]), (djt[:, :, :, 1], d_all[:, :, :, 2]),
            (gfr[:], gf_raw), (fsel[:], fselt), (bdiag, brow_w), (brow, frow), (tr[:], trig), (hm[:], hmat), (h16[:], hmat16), (mod[:], modt), (g1m[:], gavg),
            (ghm[:], ghalo), (idm[:], ident), (selm[:], sel), (sgm, sgn)]
        CONSTS = 16 * len(const_dmas)

        def turns(eng, body, peel_first=False, peel_last=False):
            lo, hi = int(peel_first), IT - int(peel_last)
            if peel_first:
                body(0)
            with eng.Fori(lo, hi) as it:
                body(it)
            if peel_last:
                body(IT - 1)

        def settle(eng):
            eng.sem_inc(s["waits_passed"], 1)

        block = ctx.enter_context(nc.Block())

        @block.sync
        def _(sp):
            for dst, src in const_dmas:
                sp.dma_start(dst, src).then_inc(s["consts_loaded"], 16)
            sp.dma_start(scratch[:, :, 6 * P:].bitcast(F16), em).then_inc(s["em_copied"], 16)
            with sp.Fori(0, IT) as it:
                for u in range(UN):
                    sp.wait_ge(s["stats_read"], it * UN + u + 1)
                    sp.dma_start(xs[:, u // 2, u % 2, 1:1 + W], x5[0, it * UN + u]).then_inc(
                        x_loaded[u // 2][u % 2], 16)
                for u in range(UN):
                    sp.wait_ge(s["wj_built"], it * UN + u + 3)
                    sp.dma_start(scratch[it * UN + u, :, 0:6 * P], wflat[:, u % 2, 0:6 * P]).then_inc(
                        w_stored[u % 2], 16)
            for u in range(2):
                sp.wait_ge(w_stored[u], 16 * (NS // 2) + 16)
            sp.wait_ge(s["em_copied"], 16)

            def image(b, more):
                def conv_turn(it):
                    first, last = isinstance(it, int) and it == 0, isinstance(it, int) and it == IT - 1
                    for v in range(2):
                        j = it * UN + 2 * v
                        sp.wait_ge(s["stats_read"], b * NS + NS + 4)
                        settle(sp)
                        sp.wait_ge(s["conv_done"], b * NS + it * UN + 2 * v + 2)
                        settle(sp)
                        for w in range(2):
                            sp.dma_start(xs[:, v, w, 1:1 + W], x5[b, j + w]).then_inc(x_loaded[v][w], 16)
                        sp.wait_ge(s["y_done"], b * NS + 2)
                        for q in range(2):
                            sp.wait_ge(y_stored[q], b * (16 * NS // 2) + 16)
                        for t in range(3):
                            c0 = 3 - t
                            top = halo[32 * t:32 * t + C, v, :, c0:c0 + W]
                            bot = halo[32 * t + C:32 * t + 2 * C, v, :, c0:c0 + W]
                            if first and v == 0:
                                tsrc = xh[b, 0].rearrange("d c n -> c d n")[:, 1:8:6]
                            else:
                                tsrc = xh[b, bass.ds(j - 1, 2), D - 1].rearrange("j c n -> c j n")
                            if last and v == 1:
                                bsrc = xh[b, NS - 1].rearrange("d c n -> c d n")[:, 0:7:6]
                            else:
                                bsrc = xh[b, bass.ds(j + 1, 2), 0].rearrange("j c n -> c j n")
                            sp.dma_start(top, tsrc).then_inc(halo_loaded[v], 16)
                            sp.dma_start(bot, bsrc).then_inc(halo_loaded[v], 16)
                turns(sp, conv_turn, peel_first=True, peel_last=True)

                def store(b, i, slot):
                    sp.wait_ge(s["y_out_ready"], b * NS + i + 1 + 2)
                    settle(sp)
                    sp.dma_start(o5[b, i], yt[:, slot]).then_inc(y_stored[slot], 16)

                sp.wait_ge(s["conv_done"], b * NS + NS + 4)
                settle(sp)

                def mix_turn(it):
                    for u in range(UN):
                        i = it * UN + u
                        sp.wait_ge(s["y_done"], b * NS + i + 1)
                        sp.dma_start(wflat[:, u % 2, 0:WJ], scratch[i]).then_inc(w_loaded[u % 2], 16)
                        if not (isinstance(it, int) and it == 0 and u < 3):
                            store(b, i - 3, (u + 1) % 2)
                        if more:
                            sp.wait_ge(s["stats_read"], b * NS + NS + i + 1)
                            sp.dma_start(xs[:, u // 2, u % 2, 1:1 + W], x5[b + 1, i]).then_inc(
                                x_loaded[u // 2][u % 2], 16)
                turns(sp, mix_turn, peel_first=True)
                for u in range(1, UN):
                    store(b, NS - UN + u, u % 2)

            with sp.Fori(0, B - 1) as b:
                image(b, True)
            image(B - 1, False)
            for q in range(2):
                sp.wait_ge(y_stored[q], B * (16 * NS // 2) + 16)

        @block.gpsimd
        def _(pool):
            pool.wait_ge(s["consts_loaded"], CONSTS)
            nc.gpsimd.memset(onesm[:], 1.0).then_inc(s["bases_built"], 1)

            with pool.Fori(0, NS // 2) as h:
                for u in range(2):
                    pool.wait_ge(s["wh_ready"], 2 * h + u + 1)
                    nc.gpsimd.tensor_tensor(w16[:, u, 0:6, 1], wf[:, u], w16[:, u, 0:6, 0], ALU.subtract).then_inc(
                        s["wj_built"], 1)

            def image(b):
                pool.wait_ge(s["y_done"], b * NS + 2)
                settle(pool)
                nc.gpsimd.memset(acc[:], 0.0).then_inc(s["acc_zeroed"], 1)
                pool.wait_ge(s["acc_zeroed"], b + 1)

                def edges(it, v, g):
                    for w in range(2):
                        pool.wait_ge(x_loaded[v][w], (2 * b * IT + IT + it + 1) * 16)
                    pool.wait_ge(halo_loaded[v], (b * IT + it + 1) * 96)
                    settle(pool)
                    nc.gpsimd.tensor_copy(xs[:, v, :, 0:XW:XW - 1], xs[:, v, :, 2:W:W - 3])
                    nc.gpsimd.tensor_copy(halo[0:32, v, :, 2:3], halo[0:32, v, :, 4:5]).then_inc(s["left_edges"], 1)
                    pool.wait_ge(s["left_edges"], b * (NS // 2) + (g + 1))
                    settle(pool)
                    nc.gpsimd.tensor_copy(halo[64:96, v, :, W + 1:W + 2],
                                          halo[64:96, v, :, W - 1:W]).then_inc(s["edges_ready"], 1)
                    pool.wait_ge(s["edges_ready"], b * (NS // 2) + (g + 1))
                    settle(pool)

                edges(0, 0, 0)

                def turn(it):
                    last = isinstance(it, int)
                    for v in range(2):
                        if not (last and v == 1):
                            edges(it + v, 1 - v, it * 2 + v + 1)
                        for w in range(2):
                            i = it * UN + 2 * v + w
                            pool.wait_ge(s["fold_done"], b * NS + i + 5)
                            pool.wait_ge(s["acc0_done"], b * NS + i + 1)
                            nc.gpsimd.tensor_tensor(acc[:, 0], acc[:, 0], x1[:, i].rearrange("k a b c -> k (a b c)"),
                                                    ALU.add).then_inc(s["acc0_done"], 1)
                turns(pool, turn, peel_last=True)

                def sin_product(k):
                    pool.wait_ge(s["x0f_ready"], k + 1)
                    nc.gpsimd.tensor_tensor(xf[:, 2, 0], xf[:, 0, 1], tr[:, 1], ALU.mult)
                    nc.gpsimd.tensor_tensor(xf[:, 2, 1], xf[:, 0, 0], tr[:, 1], ALU.mult).then_inc(s["xsf_ready"], 1)

                sin_product(b * NS)
                sin_product(b * NS + 1)
                pool.wait_ge(s["x0f_ready"], b * NS + 1)
                nc.gpsimd.tensor_tensor(x1[:, 0], x1[:, 0], bterm[:], ALU.add).then_inc(s["bias_added"], 1)
                pool.wait_ge(s["bias_added"], b + 1)
                settle(pool)

                def mix_turn(it):
                    for u in range(UN):
                        i = it * UN + u
                        k = b * NS + i
                        if not (isinstance(it, int) and u >= UN - 2):
                            sin_product(k + 2)
                        pool.wait_ge(s["yp_ready"], k + 3)
                        nc.gpsimd.tensor_tensor(yp[:, u % 2], yp[:, u % 2], x1[:, i], ALU.add).then_inc(
                            s["yr_ready"], 1)
                turns(pool, mix_turn, peel_last=True)

            with pool.Fori(0, B) as b:
                image(b)

        @block.tensor
        def _(pe):
            pe.wait_ge(s["consts_loaded"], CONSTS)
            nc.tensor.matmul(pf[:], bdiag, brow.rearrange("k a b c -> k (a b c)"), start=True, stop=True).then_inc(
                s["bterm_mm"], 1)
            pe.sem_inc(s["conv_done"], 4)
            pe.sem_inc(s["y_done"], 2)

            def image(b):
                pe.wait_ge(s["g0_aggr"], b + 1)
                nc.tensor.matmul(pstat[:, 0:1], g1m[:], col(MV0), start=True, stop=True)
                nc.tensor.matmul(pstat[0:96, 1:2], ghm[:], col(MV0), start=True, stop=True).then_inc(s["g0_mean"], 1)
                pe.wait_ge(s["g0_q"], b + 1)
                nc.tensor.matmul(pstat[:, 2:3], g1m[:], col(Q0), start=True, stop=True)
                nc.tensor.matmul(pstat[0:96, 3:4], ghm[:], col(Q0), start=True, stop=True).then_inc(s["g0_qps"], 1)
                pe.wait_ge(s["g0_pmb"], b + 1)
                nc.tensor.matmul(pstat[:, 4:4 + NX], pmb[:], fcwt[:], start=True, stop=True).then_inc(s["g0_lps"], 1)
                pe.wait_ge(s["g0_w2"], b + 1)
                for t in range(3):
                    nc.tensor.matmul(pstat[:, 8:9], wc[:, t], col(MU0), start=t == 0, stop=False)
                nc.tensor.matmul(pstat[:, 8:9], wh[:], col(MUH, 96), start=False, stop=True).then_inc(s["g0_bps"], 1)
                pe.wait_ge(s["g0_conv_weights"], b + 1)
                settle(pe)

                def conv_turn(it):
                    for u in range(UN):
                        k = b * NS + it * UN + u
                        if u % 2 == 0:
                            pe.wait_ge(s["edges_ready"], b * (NS // 2) + it * 2 + u // 2 + 1)
                        pe.wait_ge(s["fold_done"], k + 1)
                        for t in range(3):
                            nc.tensor.matmul(cps[u][:], wc[:, t], xs[:, u // 2, u % 2, t:t + W], start=t == 0, stop=False)
                        nc.tensor.matmul(cps[u][:], wh[:], halo[0:96, u // 2, u % 2, 2:2 + W],
                                         start=False, stop=True).then_inc(s["conv_done"], 1)
                turns(pe, conv_turn)

                pe.wait_ge(s["g1_m1"], b + 1)
                nc.tensor.matmul(pstat[:, 16:18], g1m[:], sm[:, M1:M1 + 2], start=True, stop=True).then_inc(s["g1_ps"], 1)
                pe.wait_ge(s["g1_acc"], b + 1)
                for t in range(3):
                    last = nc.tensor.matmul(pf[0:NF, :], selm[:, t], acc[:, t], start=t == 0, stop=t == 2)
                last.then_inc(s["g1_rps"], 1)
                pe.wait_ge(s["g1_z3"], b + 1)
                for e in range(2):
                    for a in range(3):
                        for r in range(2):
                            z = zt[:, ((e * 3 + a) * 2 + r) * NS:((e * 3 + a) * 2 + r + 1) * NS]
                            last = nc.tensor.matmul(pj[:, e * NS:(e + 1) * NS], djt[:, r, a, 1 - e], z,
                                                    start=(a, r) == (0, 0), stop=(a, r) == (2, 1))
                last.then_inc(s["g1_jps"], 1)
                pe.wait_ge(s["g1_rt"], b + 1)
                for sg in range(2):
                    for p in range(2):
                        for t in range(3):
                            last = nc.tensor.matmul(pbf[:, (2 * sg + p) * P:(2 * sg + p + 1) * P],
                                                    xf[0:NF, t, sg, p], fwt[:, 3 + t], start=t == 0, stop=t == 2)
                last.then_inc(s["g1_aps"], 1)
                pe.wait_ge(s["g1_srz"], b + 1)
                settle(pe)
                for e in range(2):
                    nc.tensor.matmul(pstat[:, 32 + e:33 + e], gfr[:, 0, 2 - 2 * e], col(SZ + 2 * e, NF), start=True,
                                     stop=False)
                    last = nc.tensor.matmul(pstat[:, 32 + e:33 + e], gfr[:, 1, 2 - 2 * e], col(SZ + 2 * e + 1, NF),
                                            start=False, stop=True)
                last.then_inc(s["g1_jfs"], 1)
                for t in range(3):
                    nc.tensor.matmul(pf[:], fwt[:, t], xf[0:NF, t].rearrange("k a b c -> k (a b c)"),
                                     start=t == 0, stop=False)
                pe.wait_ge(s["g1_bt"], b + 1)
                for sg in range(2):
                    for p in range(2):
                        o = (2 * sg + 1 - p) * P
                        last = nc.tensor.matmul(pf[:, o:o + P], btf[:, sg, p], hm[:, sg, p], start=False,
                                                stop=(sg, p) == (1, 1))
                last.then_inc(s["g1_frows"], 1)
                pe.wait_ge(s["f_ready"], b + 2)
                settle(pe)

                def mix_turn(it):
                    for u in range(UN):
                        k = b * NS + it * UN + u
                        v = u % 2
                        pe.wait_ge(s["x_ready"], k + 2)
                        pe.wait_ge(w_loaded[v], (b * (NS // 2) + it * 2 + u // 2 + 1) * 16)
                        for sg in range(2):
                            for p in range(2):
                                for n, (hs, hmv) in enumerate(PAIRS):
                                    for t in range(3):
                                        last = nc.tensor.matmul(cps[v][:, (2 * sg + p) * P:(2 * sg + p + 1) * P],
                                                                x16[:, v, t, hs, sg, p], w16[:, v, 3 + t, hmv],
                                                                start=(n, t) == (0, 0), stop=(n, t) == (2, 2))
                        last.then_inc(s["beta_done"], 1)
                        pe.wait_ge(s["yp_ready"], k + 1)
                        for n, (hs, hmv) in enumerate(PAIRS):
                            for t in range(3):
                                nc.tensor.matmul(cps[2 + v][:], w16[:, v, t, hs],
                                                 x16[:, v, t, hmv].rearrange("k a b c -> k (a b c)"),
                                                 start=(n, t) == (0, 0), stop=False)
                        nc.tensor.matmul(cps[2 + v][:], w16[:, v, 6, 0], f16[:].rearrange("k a b c -> k (a b c)"),
                                         start=False, stop=False)
                        pe.wait_ge(s["bt_ready"], k + 1)
                        for sg in range(2):
                            for p in range(2):
                                o = (2 * sg + 1 - p) * P
                                for n, (hs, hmv) in enumerate(PAIRS):
                                    last = nc.tensor.matmul(cps[2 + v][:, o:o + P], b16[:, v, hs, sg, p],
                                                            h16[:, hmv, sg, p], start=False,
                                                            stop=(sg, p, n) == (1, 1, 2))
                        last.then_inc(s["y_done"], 1)
                turns(pe, mix_turn)

            with pe.Fori(0, B) as b:
                image(b)

        @block.scalar
        def _(act):
            act.sem_inc(s["yp_ready"], 2)
            act.wait_ge(s["consts_loaded"], CONSTS)

            with act.Fori(0, NS // 2) as h:
                for u in range(2):
                    act.wait_ge(s["wf_ready"], 2 * h + u + 1)
                    act.wait_ge(w_stored[u], 16 * h + 16)
                    nc.scalar.activation(w16[:, u, 0:6, 0], wf[:, u], ACT.Copy).then_inc(s["wh_ready"], 1)

            def image(b):
                act.wait_ge(s["g0_var"], b + 1)
                nc.scalar.activation(col(SD0), col(VAR0), ACT.Sqrt)
                nc.scalar.activation(col(SDH, 96), col(TMPB, 96), ACT.Sqrt).then_inc(s["g0_sd"], 1)
                act.wait_ge(s["g0_nmax"], b + 1)
                nc.scalar.activation(small[:, 2], small[:, 1], ACT.Exp, bias=col(NMX), accum_out=col(ESUM)).then_inc(
                    s["g0_exp"], 1)
                act.wait_ge(s["g0_b2"], b + 1)

                def square(k, i):
                    act.wait_ge(s["fold_done"], k + 5)
                    act.wait_ge(s["sq_done"], k + 1)
                    nc.scalar.activation(junk[:, 0], x1[:, i, 0].rearrange("k a b -> k (a b)"), ACT.Square, bias=col(NMU0),
                                         accum_out=ssq[:, 0, bass.ds(i, 1)])
                    nc.scalar.activation(junk[:, 1], x1[:, i, 1].rearrange("k a b -> k (a b)"), ACT.Square,
                                         accum_out=ssq[:, 1, bass.ds(i, 1)]).then_inc(s["sq_done"], 1)

                def conv_turn(it):
                    for u in range(UN):
                        i = it * UN + u
                        k = b * NS + i
                        act.wait_ge(s["conv_done"], k + 5)
                        act.wait_ge(s["fold_done"], k + 3)
                        nc.scalar.activation(tmph[:, u % 2].rearrange("k p t -> k t p"),
                                             cps[u][:, HW2:W].rearrange("k (t p) -> k t p", p=2),
                                             ACT.Copy).then_inc(s["half_ready"], 1)
                        if u:
                            square(k - 1, i - 1)
                    square(b * NS + it * UN + UN - 1, it * UN + UN - 1)
                turns(act, conv_turn)

                act.wait_ge(s["g1_var"], b + 1)
                nc.scalar.activation(col(SD1), col(VAR1), ACT.Sqrt).then_inc(s["g1_sd"], 1)
                act.wait_ge(s["g1_rps"], b + 1)
                nc.scalar.activation(xf[0:NF, 0].rearrange("k a b c -> k (a b c)"), pf[0:NF, :],
                                     ACT.Copy).then_inc(s["g1_r"], 1)
                act.wait_ge(s["g1_aps"], b + 1)
                nc.scalar.activation(btf.rearrange("k a b c -> k (a b c)"), pbf[:], ACT.Copy).then_inc(s["g1_bt"], 1)
                act.wait_ge(s["g1_frows"], b + 1)
                act.wait_ge(s["g1_jf"], b + 1)
                for p in range(2):
                    nc.scalar.activation(ffull[:, 0, p], pf[:, p * P:(p + 1) * P], ACT.Identity, scale=SF,
                                         bias=col(JFE + p))
                nc.scalar.activation(ffull[:, 1].rearrange("k a b -> k (a b)"), pf[:, HW2:W], ACT.Copy,
                                     scale=SF).then_inc(s["g1_fh"], 1)
                act.wait_ge(s["g1_fh"], b + 1)
                nc.scalar.activation(f16[:], ffull, ACT.Copy).then_inc(s["g1_fl"], 1)
                act.wait_ge(s["g1_bj"], b + 1)

                def normalise(k, i):
                    act.wait_ge(s["x_ready"], k + 1)
                    nc.scalar.activation(xf[:, 0, 0], x1[:, i, 0], ACT.Identity, scale=col(RSX), bias=col(NB1))
                    nc.scalar.activation(xf[:, 0, 1], x1[:, i, 1], ACT.Copy, scale=col(RSX)).then_inc(
                        s["x0f_ready"], 1)

                def x_high(k, v):
                    act.wait_ge(s["y_done"], k + 1)
                    act.wait_ge(s["x0f_ready"], k + 1)
                    nc.scalar.activation(x16[:, v, 0, 0], xf[:, 0], ACT.Copy).then_inc(s["x0h_ready"], 1)

                def products_high(k, v):
                    act.wait_ge(s["xcf_ready"], k + 1)
                    nc.scalar.activation(x16[:, v, 1, 0], xf[:, 1], ACT.Copy).then_inc(s["xch_ready"], 1)
                    act.wait_ge(s["xsf_ready"], k + 1)
                    nc.scalar.activation(x16[:, v, 2, 0], xf[:, 2], ACT.Copy).then_inc(s["xsh_ready"], 1)

                normalise(b * NS, 0)
                x_high(b * NS, 0)
                products_high(b * NS, 0)
                normalise(b * NS + 1, 1)

                def mix_turn(it):
                    last = isinstance(it, int)
                    for u in range(UN):
                        i = it * UN + u
                        k = b * NS + i
                        v = u % 2
                        if not (last and u == UN - 1):
                            x_high(k + 1, 1 - v)
                        act.wait_ge(s["beta_done"], k + 1)
                        nc.scalar.activation(b16[:, v, 0].rearrange("k a b c -> k (a b c)"), cps[v][:], ACT.Copy,
                                             scale=SB / SY).then_inc(s["bth_ready"], 1)
                        if not (last and u == UN - 1):
                            products_high(k + 1, 1 - v)
                        if not (last and u >= UN - 2):
                            normalise(k + 2, i + 2)
                        act.wait_ge(s["y_done"], k + 3)
                        act.wait_ge(s["y_out_ready"], k + 1)
                        for p in range(2):
                            nc.scalar.activation(yp[:, v, 0, p], cps[2 + v][:, p * P:(p + 1) * P], ACT.Identity,
                                                 scale=1.0 / SY, bias=bj[:, p, bass.ds(i, 1)])
                        nc.scalar.activation(yp[:, v, 1].rearrange("k a b -> k (a b)"), cps[2 + v][:, HW2:W], ACT.Copy,
                                             scale=1.0 / SY).then_inc(s["yp_ready"], 1)
                turns(act, mix_turn, peel_last=True)

            with act.Fori(0, B) as b:
                image(b)

        @block.vector
        def _(dve):
            tt = nc.vector.tensor_tensor
            stt = nc.vector.scalar_tensor_tensor
            ts = nc.vector.tensor_scalar

            dve.sem_inc(s["stats_read"], 4)
            dve.sem_inc(s["fold_done"], 4)
            dve.sem_inc(s["y_out_ready"], 2)
            for name in ("x_ready", "s_done", "sq_done", "acc0_done", "accc_done", "accs_done", "sj_kept"):
                dve.sem_inc(s[name], 1)
            for free in (*w_stored, *y_stored):
                dve.sem_inc(free, 16)
            dve.sem_inc(s["wj_built"], 2)
            dve.sem_inc(s["f_ready"], 1)
            dve.wait_ge(s["consts_loaded"], CONSTS)

            dve.wait_ge(s["bterm_mm"], 1)
            nc.vector.tensor_copy(bterm[:].rearrange("k a b c -> k (a b c)"), pf[:])

            def gr(u, e, sign):
                return {0: [(sign, 0, 1, e)], 1: [(sign, 0, 2, e), (sign, 0, 0, e)],
                        2: [(-sign, 1, 2, e), (sign, 1, 0, e)]}[u]

            def gi(u, e, sign):
                return {0: [(sign, 1, 1, e)], 1: [(sign, 1, 2, e), (sign, 1, 0, e)],
                        2: [(sign, 0, 2, e), (-sign, 0, 0, e)]}[u]

            built = 1
            dve.wait_ge(s["bases_built"], built)
            for u in range(3):
                types = [gr(u, 1, 1), gr(u, 2, 1) + gr(u, 0, 1), gi(u, 2, -1) + gi(u, 0, 1),
                         gi(u, 1, 1), gi(u, 2, 1) + gi(u, 0, 1), gr(u, 2, 1) + gr(u, 0, -1)]
                for t, terms in enumerate(types):
                    for n, (sign, r, a, e) in enumerate(terms):
                        if n == 0:
                            ins = ts(bases[:, u, t], dall[:, r, a, e], SW * sign, None, ALU.mult)
                        else:
                            ins = stt(bases[:, u, t], dall[:, r, a, e], SW * sign, bases[:, u, t], ALU.mult, ALU.add)
                        ins.then_inc(s["bases_built"], 1)
                        built += 1
                        dve.wait_ge(s["bases_built"], built)

            def strip_weights(j, u):
                dve.wait_ge(s["wj_built"], j + 1)
                stt(wf[:, u], bases[:, 1], mod[:, 0, bass.ds(j, 1)], bases[:, 0], ALU.mult, ALU.add).then_inc(
                    s["bases_built"], 1)
                dve.wait_ge(s["bases_built"], built + 1 + j)
                stt(wf[:, u], bases[:, 2], mod[:, 1, bass.ds(j, 1)], wf[:, u], ALU.mult, ALU.add).then_inc(
                    s["wf_ready"], 1)

            def stats(i, v, w, count):
                dve.wait_ge(x_loaded[v][w], count * 16)
                nc.vector.bn_stats(bst[:, i], xs[:, v, w, 1:1 + W]).then_inc(s["stats_read"], 1)

            with dve.Fori(0, IT) as it:
                for u in range(UN):
                    strip_weights(it * UN + u, u % 2)
                    stats(it * UN + u, u // 2, u % 2, it + 1)

            base = built + NS
            for r in range(2):
                for e in range(3):
                    tt(gfr[:, r, e], gfr[:, r, e], sgm[:, r], ALU.mult).then_inc(s["bases_built"], 1)
            dve.wait_ge(s["bases_built"], base + 6)
            nc.vector.tensor_copy(fwt[:, 0], gfr[:, 0, 1])
            tt(fwt[:, 1], gfr[:, 0, 2], gfr[:, 0, 0], ALU.add)
            tt(fwt[:, 2], gfr[:, 1, 0], gfr[:, 1, 2], ALU.subtract)
            nc.vector.tensor_copy(fwt[:, 3], gfr[:, 1, 1])
            tt(fwt[:, 4], gfr[:, 1, 2], gfr[:, 1, 0], ALU.add)
            tt(fwt[:, 5], gfr[:, 0, 2], gfr[:, 0, 0], ALU.subtract)

            def image(b, more):
                n = b + 1
                dve.wait_ge(s["stats_read"], b * NS + NS + 4)
                settle(dve)
                nc.vector.bn_aggr(sm[:, MV0:MV0 + 2], bst[:].rearrange("k a b -> k (a b)")).then_inc(s["g0_aggr"], 1)
                dve.wait_ge(s["g0_mean"], n)
                nc.vector.tensor_copy(col(MU0), pstat[:, 0:1])
                nc.vector.tensor_copy(col(MUH, 96), pstat[0:96, 1:2]).then_inc(s["g0_mu"], 1)
                dve.wait_ge(s["g0_mu"], n)
                tt(col(DEV), col(MV0), col(MU0), ALU.subtract)
                ts(col(NMU0), col(MU0), -1.0, None, ALU.mult).then_inc(s["g0_dev"], 1)
                dve.wait_ge(s["g0_dev"], n)
                stt(col(Q0), col(DEV), col(DEV), col(MV1), ALU.mult, ALU.add).then_inc(s["g0_q"], 1)
                dve.wait_ge(s["g0_qps"], n)
                ts(col(VAR0), pstat[:, 2:3], EPS, None, ALU.add)
                ts(col(TMPB, 96), pstat[0:96, 3:4], EPS, None, ALU.add).then_inc(s["g0_var"], 1)
                dve.wait_ge(s["g0_sd"], n)
                nc.vector.reciprocal(col(RS0), col(SD0))
                nc.vector.reciprocal(col(RSH, 96), col(SDH, 96)).then_inc(s["g0_rs"], 1)
                dve.wait_ge(s["g0_rs"], n)
                ts(col(PM), col(DEV), col(RS0), 1.0 / D, ALU.mult, ALU.mult).then_inc(s["g0_pm"], 1)
                dve.wait_ge(s["g0_pm"], n)
                ts(pmb[:], onesm[:], col(PM), None, ALU.mult).then_inc(s["g0_pmb"], 1)
                dve.wait_ge(s["g0_lps"], n)
                tt(small[:, 1], pstat[:, 4:4 + NX], fcbt[:], ALU.add).then_inc(s["g0_logit"], 1)
                dve.wait_ge(s["g0_logit"], n)
                nc.vector.reduce_max(col(MXL), small[:, 1], AX_X).then_inc(s["g0_max"], 1)
                dve.wait_ge(s["g0_max"], n)
                ts(col(NMX), col(MXL), -1.0, None, ALU.mult).then_inc(s["g0_nmax"], 1)
                dve.wait_ge(s["g0_exp"], n)
                nc.vector.reciprocal(col(RSUM), col(ESUM)).then_inc(s["g0_rsum"], 1)
                dve.wait_ge(s["g0_rsum"], n)
                ts(small[:, 3], small[:, 2], col(RSUM), None, ALU.mult).then_inc(s["g0_route"], 1)
                dve.wait_ge(s["g0_route"], n)
                ts(small[:, 4], small[:, 3], col(RS0), 0.5, ALU.mult, ALU.mult)
                ts(small[0:96, 5], small[0:96, 3], col(RSH, 96), 0.5, ALU.mult, ALU.mult).then_inc(s["g0_scal"], 1)
                dve.wait_ge(s["g0_scal"], n)
                wcf = wc[:].rearrange("k a b -> k (a b)")
                ts(wcf, emain[:, 0], small[:, 4, 0:1], None, ALU.mult)
                ts(wh[:], ehalo[:, 0], small[0:96, 5, 0:1], None, ALU.mult).then_inc(s["g0_w0"], 1)
                dve.wait_ge(s["g0_w0"], n)
                stt(wcf, emain[:, 1], small[:, 4, 1:2], wcf, ALU.mult, ALU.add)
                stt(wh[:], ehalo[:, 1], small[0:96, 5, 1:2], wh[:], ALU.mult, ALU.add).then_inc(s["g0_w1"], 1)
                dve.wait_ge(s["g0_w1"], n)
                stt(wcf, emain[:, 2], small[:, 4, 2:3], wcf, ALU.mult, ALU.add)
                stt(wh[:], ehalo[:, 2], small[0:96, 5, 2:3], wh[:], ALU.mult, ALU.add).then_inc(s["g0_w2"], 1)
                dve.wait_ge(s["g0_bps"], n)
                stt(wc[:, 1], idm[:], 0.5, wc[:, 1], ALU.mult, ALU.add).then_inc(s["g0_conv_weights"], 1)
                stt(col(B2), pstat[:, 8:9], -2.0, biast[:], ALU.mult, ALU.add).then_inc(s["g0_b2"], 1)
                dve.wait_ge(s["g0_b2"], n)
                dve.wait_ge(s["acc_zeroed"], n)
                settle(dve)

                def conv_turn(it):
                    for u in range(UN):
                        i = it * UN + u
                        k = b * NS + i
                        first = cps[u][:, 0:HW2].rearrange("k (t p) -> k p t", p=2)
                        second = tmph[:, u % 2]
                        dve.wait_ge(s["half_ready"], k + 1)
                        stt(x1[:, i, 0], first, col(B2), second, ALU.add, ALU.add)
                        tt(x1[:, i, 1], first, second, ALU.subtract).then_inc(s["fold_done"], 1)
                        dve.wait_ge(s["fold_done"], k + 5)
                        xf = x1[:, i].rearrange("k a b c -> k (a b c)")
                        dve.wait_ge(s["accc_done"], k + 1)
                        stt(acc[:, 1], xf, mod[:, 0, bass.ds(i, 1)], acc[:, 1], ALU.mult, ALU.add).then_inc(
                            s["accc_done"], 1)
                        dve.wait_ge(s["accs_done"], k + 1)
                        stt(acc[:, 2], xf, mod[:, 1, bass.ds(i, 1)], acc[:, 2], ALU.mult, ALU.add).then_inc(
                            s["accs_done"], 1)
                        dve.wait_ge(s["s_done"], k + 1)
                        if u == 0:
                            dve.wait_ge(s["sj_kept"], b * IT + it + 1)
                        for t in range(2):
                            for p in range(2):
                                last = stt(junk2[:, 2 * t + p], x1[:, i, 1, p], 1.0, tr[:, t, p], ALU.mult, ALU.mult,
                                           accum_out=sjt[:, 2 * t + p, u:u + 1])
                        last.then_inc(s["s_done"], 1)
                    dve.wait_ge(s["s_done"], b * NS + it * UN + UN + 1)
                    nc.vector.tensor_copy(sj[:, :, bass.ds(it * UN, UN)], sjt[:]).then_inc(s["sj_kept"], 1)
                turns(dve, conv_turn)

                dve.wait_ge(s["acc0_done"], b * NS + NS + 1)
                dve.wait_ge(s["accc_done"], b * NS + NS + 1)
                dve.wait_ge(s["accs_done"], b * NS + NS + 1)
                dve.wait_ge(s["sj_kept"], b * IT + IT + 1)
                dve.wait_ge(s["sq_done"], b * NS + NS + 1)
                nc.vector.reduce_sum(col(SUMA), acc[:, 0, 0:HW2], AX_X)
                nc.vector.reduce_sum(col(DM), ssq[:].rearrange("k a b -> k (a b)"), AX_X).then_inc(s["g1_sum"], 1)
                dve.wait_ge(s["g1_sum"], n)
                ts(col(M1), col(SUMA), 2.0 / (NS * W), None, ALU.mult)
                ts(col(Q1), col(DM), 2.0 / (NS * W), None, ALU.mult).then_inc(s["g1_m1"], 1)
                dve.wait_ge(s["g1_ps"], n)
                nc.vector.tensor_copy(sm[:, MU1:MU1 + 2], pstat[:, 16:18]).then_inc(s["g1_mu"], 1)
                dve.wait_ge(s["g1_mu"], n)
                tt(col(DM), col(MU1), col(MU0), ALU.subtract).then_inc(s["g1_dmu"], 1)
                dve.wait_ge(s["g1_dmu"], n)
                tt(col(DM), col(DM), col(DM), ALU.mult).then_inc(s["g1_dmu2"], 1)
                dve.wait_ge(s["g1_dmu2"], n)
                ts(col(VAR1), col(E1), col(DM), EPS, ALU.subtract, ALU.add).then_inc(s["g1_var"], 1)
                dve.wait_ge(s["g1_sd"], n)
                nc.vector.reciprocal(col(RS1), col(SD1)).then_inc(s["g1_rs"], 1)
                dve.wait_ge(s["g1_rs"], n)
                tt(col(NB1), col(MU1), col(RS1), ALU.mult)
                ts(col(RSX), col(RS1), SX, None, ALU.mult)
                ts(col(KJ), col(RS1), -2.0 / W, None, ALU.mult).then_inc(s["g1_k"], 1)
                dve.wait_ge(s["g1_k"], n)
                ts(col(ACB), col(NB1), -1.0 * NS, None, ALU.mult).then_inc(s["g1_scal"], 1)
                dve.wait_ge(s["g1_scal"], n)
                ts(col(NB1), col(NB1), -SX, None, ALU.mult)
                ts(acc[:, 0, 0:HW2], acc[:, 0, 0:HW2], col(RS1), col(ACB), ALU.mult, ALU.add)
                ts(acc[:, 0, HW2:W], acc[:, 0, HW2:W], col(RS1), None, ALU.mult)
                accf = acc[:, 1:3].rearrange("k a b -> k (a b)")
                ts(accf, accf, col(RS1), None, ALU.mult).then_inc(s["g1_acc"], 1)

                sjf = sj[:].rearrange("k (t p) j -> k t p j", p=2)
                q = zt[:, 12 * NS:24 * NS].rearrange("k (a j) -> k a j", j=NS)
                z = zt[:, 0:12 * NS].rearrange("k (e a r j) -> k e a r j", e=2, a=3, r=2)
                for t in range(2):
                    stt(q[:, t], sjf[:, t, 0], 1.0, sjf[:, t, 1], ALU.mult, ALU.add)
                    last = stt(q[:, 2 + t], sjf[:, t, 0], 1.0, sjf[:, t, 1], ALU.mult, ALU.subtract)
                last.then_inc(s["g1_z1"], 1)
                dve.wait_ge(s["g1_z1"], n)
                for e in range(2):
                    ts(z[:, e, 1, 0], q[:, 2 * e], col(KJ), None, ALU.mult)
                    last = ts(z[:, e, 1, 1], q[:, 2 * e + 1], col(KJ), (-1.0, 1.0)[e], ALU.mult, ALU.mult)
                last.then_inc(s["g1_z2"], 1)
                dve.wait_ge(s["g1_z2"], n)
                for e in range(2):
                    for r in range(2):
                        for t in range(2):
                            last = tt(q[:, 4 + 4 * e + 2 * r + t], z[:, e, 1, r], mod[:, t], ALU.mult)
                last.then_inc(s["g1_zmod"], 1)
                dve.wait_ge(s["g1_zmod"], n)
                for e in range(2):
                    cr, sr, ci, si = (q[:, 4 + 4 * e + t] for t in range(4))
                    tt(z[:, e, 2, 0], cr, si, ALU.add)
                    tt(z[:, e, 2, 1], ci, sr, ALU.subtract)
                    tt(z[:, e, 0, 0], cr, si, ALU.subtract)
                    last = tt(z[:, e, 0, 1], ci, sr, ALU.add)
                last.then_inc(s["g1_z3"], 1)

                dve.wait_ge(s["g1_r"], n)
                for t in range(2):
                    for p in range(2):
                        nc.vector.tensor_tensor_reduce(
                            out=xf[0:NF, 1 + t, 0, p], in0=xf[0:NF, 0, 1, p], in1=tr[0:NF, t, p], scale=1.0,
                            scalar=0.0, op0=ALU.mult, op1=ALU.add, accum_out=col(SR + 2 * t + p, NF))
                    last = tt(xf[0:NF, 1 + t, 1], xf[0:NF, 0, 0], tr[0:NF, t], ALU.mult)
                last.then_inc(s["g1_rt"], 1)
                dve.wait_ge(s["g1_rt"], n)
                for e in range(2):
                    op = (ALU.add, ALU.subtract)[e]
                    stt(col(SZ + 2 * e, NF), col(SR, NF), 1.0, col(SR + 1, NF), ALU.mult, op)
                stt(col(SZ + 3, NF), col(SR + 2, NF), 1.0, col(SR + 3, NF), ALU.mult, ALU.subtract)
                stt(col(SZ + 1, NF), col(SR + 2, NF), 1.0, col(SR + 3, NF), ALU.mult, ALU.add).then_inc(
                    s["g1_srsum"], 1)
                dve.wait_ge(s["g1_srsum"], n)
                ts(col(SZ + 1, NF), col(SZ + 1, NF), -1.0, None, ALU.mult).then_inc(s["g1_srz"], 1)
                dve.wait_ge(s["g1_jps"], n)
                nc.vector.tensor_copy(q[:, 0], pj[:, 0:NS]).then_inc(s["g1_jt"], 1)
                dve.wait_ge(s["g1_jt"], n)
                tt(bj[:, 0], pj[:, NS:2 * NS], q[:, 0], ALU.add)
                stt(bj[:, 1], pj[:, NS:2 * NS], -1.0, q[:, 0], ALU.mult, ALU.add).then_inc(s["g1_bj"], 1)
                dve.wait_ge(s["g1_jfs"], n)
                nc.vector.tensor_copy(sm[:, SR:SR + 2], pstat[:, 32:34]).then_inc(s["g1_jfc"], 1)
                dve.wait_ge(s["g1_jfc"], n)
                stt(col(JFE), col(SR), 1.0, col(SR + 1), ALU.mult, ALU.add)
                stt(col(JFO), col(SR), 1.0, col(SR + 1), ALU.mult, ALU.subtract).then_inc(s["g1_jfsum"], 1)
                dve.wait_ge(s["g1_jfsum"], n)
                ts(sm[:, JFE:JFE + 2], sm[:, JFE:JFE + 2], -2.0 * SF / W, None, ALU.mult).then_inc(s["g1_jf"], 1)
                dve.wait_ge(s["g1_fl"], n)
                stt(flow, ffull, 1.0, f16[:], ALU.mult, ALU.subtract)
                ts(fhigh, f16[:], fsel[:, 0:1], None, ALU.mult).then_inc(s["g1_fm"], 1)
                dve.wait_ge(s["g1_fm"], n)
                stt(f16[:], flow, fsel[:, 1:2], fhigh, ALU.mult, ALU.add).then_inc(s["f_ready"], 1)

                def cos_product(k):
                    dve.wait_ge(s["x0f_ready"], k + 1)
                    tt(xf[:, 1, 0], xf[:, 0, 1], tr[:, 0], ALU.mult)
                    tt(xf[:, 1, 1], xf[:, 0, 0], tr[:, 0], ALU.mult).then_inc(s["xcf_ready"], 1)

                def x_low(k, v):
                    dve.wait_ge(s["x0h_ready"], k + 1)
                    tt(x16[:, v, 0, 1], xf[:, 0], x16[:, v, 0, 0], ALU.subtract)

                def products_low(k, v):
                    dve.wait_ge(s["xcf_ready"], k + 1)
                    dve.wait_ge(s["xch_ready"], k + 1)
                    tt(x16[:, v, 1, 1], xf[:, 1], x16[:, v, 1, 0], ALU.subtract)
                    dve.wait_ge(s["xsh_ready"], k + 1)
                    tt(x16[:, v, 2, 1], xf[:, 2], x16[:, v, 2, 0], ALU.subtract).then_inc(s["x_ready"], 1)

                cos_product(b * NS)
                x_low(b * NS, 0)
                products_low(b * NS, 0)
                cos_product(b * NS + 1)

                def unfold(k, v, stored):
                    dve.wait_ge(s["yr_ready"], k + 1)
                    dve.wait_ge(y_stored[v], stored)
                    yv = yt[:, v].rearrange("k (q t p) -> k q p t", q=2, p=2)
                    tt(yv[:, 0], yp[:, v, 0], yp[:, v, 1], ALU.add)
                    tt(yv[:, 1], yp[:, v, 0], yp[:, v, 1], ALU.subtract).then_inc(s["y_out_ready"], 1)

                def mix_turn(it):
                    first, last = isinstance(it, int) and it == 0, isinstance(it, int) and it == IT - 1
                    for u in range(UN):
                        i = it * UN + u
                        k = b * NS + i
                        v = u % 2
                        if not (last and u == UN - 1):
                            x_low(k + 1, 1 - v)
                        dve.wait_ge(s["bth_ready"], k + 1)
                        stt(b16[:, v, 1].rearrange("k a b c -> k (a b c)"), cps[v][:], SB / SY,
                            b16[:, v, 0].rearrange("k a b c -> k (a b c)"), ALU.mult, ALU.subtract).then_inc(
                            s["bt_ready"], 1)
                        if not (last and u == UN - 1):
                            products_low(k + 1, 1 - v)
                        if not (first and u == 0):
                            unfold(k - 1, 1 - v, (b * (NS // 2) + it * 2 + (u - 1) // 2 + 1) * 16)
                        if more:
                            stats(i, u // 2, u % 2, 2 * b * IT + 2 * IT + it + 1)
                        if not (last and u >= UN - 2):
                            cos_product(k + 2)
                turns(dve, mix_turn, peel_first=True, peel_last=True)
                unfold(b * NS + NS - 1, 1, ((b + 1) * (NS // 2)) * 16)

            with dve.Fori(0, B - 1) as b:
                image(b, True)
            image(B - 1, False)


def kernel(x, L0_conv_w_experts, L0_conv_bias, L0_conv_fc_w, L0_conv_fc_b, L1_conv_w_real, L1_conv_w_imag,
           L1_conv_b_real, L1_conv_b_imag):
    import numpy as np
    import concourse.bacc as bacc
    from concourse.bass_utils import run_bass_kernel_spmd

    f32 = np.float32
    x = np.ascontiguousarray(x)
    we, wr, wi = (np.asarray(a) for a in (L0_conv_w_experts, L1_conv_w_real, L1_conv_w_imag))
    a = {"x": x}

    em = np.zeros((C, D, NX, 3, C, D), f32)
    eh = np.zeros((3, 2, C, NX, C, D), f32)
    for t in range(3):
        for d_in in range(D):
            for d_out in range(D):
                if 0 <= d_in - d_out + 1 <= 2:
                    em[:, d_in, :, t, :, d_out] = we[:, :, :, d_in - d_out + 1, t].transpose(2, 0, 1)
        eh[t, 0, :, :, :, 0] = we[:, :, :, 0, t].transpose(2, 0, 1)
        eh[t, 1, :, :, :, D - 1] = we[:, :, :, 2, t].transpose(2, 0, 1)
    a["e_main"] = em.reshape(P, NX, 3 * P)
    a["e_halo"] = eh.reshape(96, NX, P)
    a["bias"] = np.repeat(np.asarray(L0_conv_bias), D).reshape(P, 1)
    a["fcw"] = np.repeat(np.asarray(L0_conv_fc_w).T, D, axis=0).copy()
    a["fcb"] = np.tile(np.asarray(L0_conv_fc_b).reshape(1, NX), (P, 1))

    da = np.zeros((C, D, 2, 3, 3, C, D), f32)
    for r, w in enumerate((wr, wi)):
        for d in range(D):
            da[:, d, r, :, :, :, d] = w.transpose(0, 2, 3, 1)
    a["d_all"] = da.reshape(P, 2, 3, 3, P)

    forder = (1, 2, 1, 2, 1, 2, 0, 0)
    gf = np.zeros((3, C, 2, 3, 8, C), f32)
    sg = np.zeros((3, C, 2, 8, C), f32)
    parts = (wr, wi)
    for g, kind in enumerate(forder):
        for r in range(2):
            for t, f, part, tap, sign in ((1, 0, r, 2, 1), (2, 0, 1 - r, 2, (-1, 1)[r]), (0, 1, r, 0, 1),
                                          (0, 2, 1 - r, 0, (1, -1)[r])):
                if f == kind:
                    gf[t, :, r, :, g, :] = parts[part][:, :, tap, :].transpose(0, 2, 1)
                    sg[t, :, r, g, :] = sign * (-1.0 / W)
    a["gf_raw"] = gf.reshape(NF, 2, 3, P)
    a["sgn"] = sg.reshape(NF, 2, P)
    a["fselt"] = np.repeat(np.array([[1, 0], [1, 0], [0, 1], [0, 1], [1, 0], [1, 0], [1, 0], [0, 1]], f32), C, axis=0)

    theta = 2 * np.pi / W
    rows = theta * np.arange(W).reshape(NS, D)
    full = (SY / SF) * np.stack([np.ones((NS, D)), np.cos(rows), np.sin(rows)])
    high = full.astype(np.float16)
    low = (full - high).astype(np.float16)
    pl = np.zeros((NS, 8, C, C, D), np.float16)
    for g, (kind, values) in enumerate(zip(forder, (high, high, high, high, low, low, high, high))):
        for o in range(C):
            pl[:, g, o, o] = values[kind]
    a["em"] = pl.reshape(NS, P, P)
    bw = np.zeros((32, C, D), f32)
    for o in range(C):
        bw[o, o, 0] = np.asarray(L1_conv_b_real)[o]
        bw[C + o, o, 0] = np.asarray(L1_conv_b_imag)[o]
    a["brow_w"] = bw.reshape(32, P)

    def hilbert(d):
        d = np.asarray(d)
        out = np.zeros(d.shape)
        odd = d % 2 != 0
        out[odd] = (2.0 / W) / np.tan(np.pi * d[odd] / W)
        return out

    n = 2 * np.arange(128)[None, :] + np.arange(2)[:, None]
    fr = np.zeros((32, 2, 2, P), f32)
    fr[0:16, :, 0, 0] = 0.5
    fr[16:32, 0] = -0.5 * (hilbert(n) + hilbert(n + HW2))
    fr[16:32, 1] = -0.5 * (hilbert(n) - hilbert(n + HW2))
    a["frow"] = fr
    a["trig"] = np.broadcast_to(np.stack([np.cos(theta * n), np.sin(theta * n)]).astype(f32), (P, 2, 2, P)).copy()
    hmat = np.zeros((P, 2, 2, P), f32)
    half = np.arange(P)
    for p in range(2):
        d = 2 * (half[None, :] - half[:, None]) + (1 - p) - p
        hmat[:, 0, p] = -(hilbert(d) + hilbert(d + HW2))
        hmat[:, 1, p] = -(hilbert(d) - hilbert(d + HW2))
    a["hmat"] = hmat
    high = (SH * hmat.astype(np.float64)).astype(np.float16)
    low = (SH * hmat.astype(np.float64) - high).astype(np.float16)
    a["hmat16"] = np.stack([high, low], 1)
    md = np.stack([np.cos(rows.T), np.sin(rows.T)], 1).astype(f32)
    a["modt"] = np.tile(md, (C, 1, 1))
    grp = np.arange(P) // (2 * D)
    a["gavg"] = ((grp[:, None] == grp[None, :]) / (2.0 * D)).astype(f32)
    hgrp = (np.arange(96) % C) // 2
    a["ghalo"] = ((grp[:, None] == hgrp[None, :]) / (2.0 * D)).astype(f32)
    a["ident"] = np.eye(P, dtype=f32)
    sel = np.zeros((C, D, 3, 3, C), f32)
    for t in range(3):
        for c in range(C):
            sel[c, :, t, t, c] = 1.0
    a["sel"] = sel.reshape(P, 3, NF)

    nc = bacc.Bacc("TRN2", target_bir_lowering=False, num_devices=1, dynamic_dma_scratch_size=4096)
    aps = {k: nc.dram_tensor(f"in_{k}", v.shape, mybir.dt.from_np(v.dtype), kind="ExternalInput").ap() for k, v in a.items()}
    out = nc.dram_tensor("out", x.shape, F32, kind="ExternalOutput").ap()
    emit(nc, out=out, **aps)
    r = run_bass_kernel_spmd(nc, [{f"in_{k}": v for k, v in a.items()}], core_ids=[0])
    return r.results[0]["out"]
```
